# Optimizing a Trainium2 kernel written in Bass

```python
import numpy as np
import jax
import jax.numpy as jnp

def _softmax(x, axis=-1):
    return jax.nn.softmax(x, axis=axis)

def _gelu(x):
    return jax.nn.gelu(x, approximate=True)

def _silu(x):
    return jax.nn.silu(x)

def _sigmoid(x):
    return jax.nn.sigmoid(x)

def _layernorm(x, axis=-1, eps=1e-05):
    m = jnp.mean(x, axis=axis, keepdims=True)
    v = jnp.var(x, axis=axis, keepdims=True)
    return (x - m) / jnp.sqrt(v + eps)

def _scatter_add(tgt, idx, src, axis=0):
    return tgt.at[idx].add(src)

def _segment_sum(src, seg, n):
    return jax.ops.segment_sum(src, seg, n)
kernel_name = 'mk_prb_d1_jaxref_r8_dde385'

def setup_inputs(seed: int=0):
    np.random.seed(seed)
    _w = jnp.asarray

    def _L0_attn_setup():
        import jax, jax.numpy as jnp
        import numpy as np
        N, L, D, A, F, B = (4, 512, 128, 128, 512, 8)
        EPS_LN = 1e-06
        EPS_Z = 1e-06

        def _layernorm(x, scale, bias):
            m = jnp.mean(x, axis=-1, keepdims=True)
            v = jnp.mean(jnp.square(x - m), axis=-1, keepdims=True)
            return (x - m) * jax.lax.rsqrt(v + EPS_LN) * scale + bias

        def _block(x, p):
            Wq, bq, Wk, bk, Wv, bv, Wo, bo, ln1_s, ln1_b, Wf1, bf1, Wf2, bf2, ln2_s, ln2_b = p
            residual = x
            q = jnp.einsum('nld,da->nla', x, Wq) + bq
            k = jnp.einsum('nld,da->nla', x, Wk) + bk
            v = jnp.einsum('nld,da->nla', x, Wv) + bv
            Q = jax.nn.elu(q) + 1.0
            K = jax.nn.elu(k) + 1.0
            KV = jnp.einsum('nsh,nsh->nh', K, v)
            Ksum = jnp.sum(K, axis=1)
            Z = 1.0 / (Q * Ksum[:, None, :] + EPS_Z)
            V = Q * KV[:, None, :] * Z
            attn = jax.nn.gelu(jnp.einsum('nla,ad->nld', V, Wo) + bo)
            x = _layernorm(attn + residual, ln1_s, ln1_b)
            residual = x
            h = jax.nn.gelu(jnp.einsum('nld,df->nlf', x, Wf1) + bf1)
            ff = jax.nn.gelu(jnp.einsum('nlf,fd->nld', h, Wf2) + bf2)
            x = _layernorm(ff + residual, ln2_s, ln2_b)
            return (x, None)
        key = jax.random.key(seed)
        ks = jax.random.split(key, 10)
        s = 0.02
        x = jax.random.normal(ks[0], (N, L, D), dtype=jnp.float32)
        Wq = jax.random.normal(ks[1], (B, D, A), dtype=jnp.float32) * s
        Wk = jax.random.normal(ks[2], (B, D, A), dtype=jnp.float32) * s
        Wv = jax.random.normal(ks[3], (B, D, A), dtype=jnp.float32) * s
        Wo = jax.random.normal(ks[4], (B, A, D), dtype=jnp.float32) * s
        Wf1 = jax.random.normal(ks[5], (B, D, F), dtype=jnp.float32) * s
        Wf2 = jax.random.normal(ks[6], (B, F, D), dtype=jnp.float32) * s
        return {'x': x, 'Wq': Wq, 'bq': jnp.zeros((B, A), jnp.float32), 'Wk': Wk, 'bk': jnp.zeros((B, A), jnp.float32), 'Wv': Wv, 'bv': jnp.zeros((B, A), jnp.float32), 'Wo': Wo, 'bo': jnp.zeros((B, D), jnp.float32), 'ln1_s': jnp.ones((B, D), jnp.float32), 'ln1_b': jnp.zeros((B, D), jnp.float32), 'Wf1': Wf1, 'bf1': jnp.zeros((B, F), jnp.float32), 'Wf2': Wf2, 'bf2': jnp.zeros((B, D), jnp.float32), 'ln2_s': jnp.ones((B, D), jnp.float32), 'ln2_b': jnp.zeros((B, D), jnp.float32)}
    _L0_attn_in = _L0_attn_setup()

    def _L0_ffn_setup():
        import jax, jax.numpy as jnp
        import numpy as np
        B, S, D, E, F = (2, 256, 128, 8, 512)
        key = jax.random.key(seed)
        ks = jax.random.split(key, 4)
        return {'hidden_states': jax.random.normal(ks[0], (B, S, D), dtype=jnp.float32), 'Wr': jax.random.normal(ks[1], (D, E), dtype=jnp.float32) * (1.0 / np.sqrt(D)), 'W1': jax.random.normal(ks[2], (E, D, F), dtype=jnp.float32) * (1.0 / np.sqrt(D)), 'b1': jnp.zeros((E, F), dtype=jnp.float32), 'W2': jax.random.normal(ks[3], (E, F, D), dtype=jnp.float32) * (1.0 / np.sqrt(F)), 'b2': jnp.zeros((E, D), dtype=jnp.float32)}
    _L0_ffn_in = _L0_ffn_setup()
    _d = {'L0_attn_x': _L0_attn_in['x'], 'L0_attn_Wq': _L0_attn_in['Wq'], 'L0_attn_bq': _L0_attn_in['bq'], 'L0_attn_Wk': _L0_attn_in['Wk'], 'L0_attn_bk': _L0_attn_in['bk'], 'L0_attn_Wv': _L0_attn_in['Wv'], 'L0_attn_bv': _L0_attn_in['bv'], 'L0_attn_Wo': _L0_attn_in['Wo'], 'L0_attn_bo': _L0_attn_in['bo'], 'L0_attn_ln1_s': _L0_attn_in['ln1_s'], 'L0_attn_ln1_b': _L0_attn_in['ln1_b'], 'L0_attn_Wf1': _L0_attn_in['Wf1'], 'L0_attn_bf1': _L0_attn_in['bf1'], 'L0_attn_Wf2': _L0_attn_in['Wf2'], 'L0_attn_bf2': _L0_attn_in['bf2'], 'L0_attn_ln2_s': _L0_attn_in['ln2_s'], 'L0_attn_ln2_b': _L0_attn_in['ln2_b'], 'L0_ffn_Wr': _L0_ffn_in['Wr'], 'L0_ffn_W1': _L0_ffn_in['W1'], 'L0_ffn_b1': _L0_ffn_in['b1'], 'L0_ffn_W2': _L0_ffn_in['W2'], 'L0_ffn_b2': _L0_ffn_in['b2']}
    _x0 = _d['L0_attn_x']
    _d['L0_attn_x'] = jax.random.normal(jax.random.fold_in(jax.random.key(seed), 1), (2, 2048, 128), dtype=_x0.dtype)
    del _x0
    return _d

def reference(L0_attn_x, L0_attn_Wq, L0_attn_bq, L0_attn_Wk, L0_attn_bk, L0_attn_Wv, L0_attn_bv, L0_attn_Wo, L0_attn_bo, L0_attn_ln1_s, L0_attn_ln1_b, L0_attn_Wf1, L0_attn_bf1, L0_attn_Wf2, L0_attn_bf2, L0_attn_ln2_s, L0_attn_ln2_b, L0_ffn_Wr, L0_ffn_W1, L0_ffn_b1, L0_ffn_W2, L0_ffn_b2):

    def _L0_attn_ref(x, Wq, bq, Wk, bk, Wv, bv, Wo, bo, ln1_s, ln1_b, Wf1, bf1, Wf2, bf2, ln2_s, ln2_b):
        import jax, jax.numpy as jnp
        import numpy as np
        N, L, D, A, F, B = (4, 512, 128, 128, 512, 8)
        EPS_LN = 1e-06
        EPS_Z = 1e-06

        def _layernorm(x, scale, bias):
            m = jnp.mean(x, axis=-1, keepdims=True)
            v = jnp.mean(jnp.square(x - m), axis=-1, keepdims=True)
            return (x - m) * jax.lax.rsqrt(v + EPS_LN) * scale + bias

        def _block(x, p):
            Wq, bq, Wk, bk, Wv, bv, Wo, bo, ln1_s, ln1_b, Wf1, bf1, Wf2, bf2, ln2_s, ln2_b = p
            residual = x
            q = jnp.einsum('nld,da->nla', x, Wq) + bq
            k = jnp.einsum('nld,da->nla', x, Wk) + bk
            v = jnp.einsum('nld,da->nla', x, Wv) + bv
            Q = jax.nn.elu(q) + 1.0
            K = jax.nn.elu(k) + 1.0
            KV = jnp.einsum('nsh,nsh->nh', K, v)
            Ksum = jnp.sum(K, axis=1)
            Z = 1.0 / (Q * Ksum[:, None, :] + EPS_Z)
            V = Q * KV[:, None, :] * Z
            attn = jax.nn.gelu(jnp.einsum('nla,ad->nld', V, Wo) + bo)
            x = _layernorm(attn + residual, ln1_s, ln1_b)
            residual = x
            h = jax.nn.gelu(jnp.einsum('nld,df->nlf', x, Wf1) + bf1)
            ff = jax.nn.gelu(jnp.einsum('nlf,fd->nld', h, Wf2) + bf2)
            x = _layernorm(ff + residual, ln2_s, ln2_b)
            return (x, None)
        params = (Wq, bq, Wk, bk, Wv, bv, Wo, bo, ln1_s, ln1_b, Wf1, bf1, Wf2, bf2, ln2_s, ln2_b)
        out, _ = jax.lax.scan(_block, x, params)
        return out

    def _L0_ffn_ref(hidden_states, Wr, W1, b1, W2, b2):
        import jax, jax.numpy as jnp
        import numpy as np
        B, S, D, E, F = (2, 256, 128, 8, 512)
        b, s, d = hidden_states.shape
        e = Wr.shape[1]
        x = hidden_states.reshape(b * s, d)
        router_logits = x @ Wr
        router_probs = jax.nn.softmax(router_logits, axis=-1)
        expert_idx = jnp.argmax(router_probs, axis=-1)
        p_max = jnp.max(router_probs, axis=-1, keepdims=True)

        def expert_mlp(w1, bb1, w2, bb2):
            h = jax.nn.gelu(x @ w1 + bb1, approximate=False)
            return h @ w2 + bb2
        outs = jax.vmap(expert_mlp)(W1, b1, W2, b2)
        onehot = jax.nn.one_hot(expert_idx, e, dtype=x.dtype)
        next_states = jnp.einsum('te,etd->td', onehot, outs)
        out = p_max * next_states
        return out.reshape(b, s, d)
    x = L0_attn_x
    xn = _layernorm(x, axis=-1)
    x = x + _L0_attn_ref(xn, L0_attn_Wq, L0_attn_bq, L0_attn_Wk, L0_attn_bk, L0_attn_Wv, L0_attn_bv, L0_attn_Wo, L0_attn_bo, L0_attn_ln1_s, L0_attn_ln1_b, L0_attn_Wf1, L0_attn_bf1, L0_attn_Wf2, L0_attn_bf2, L0_attn_ln2_s, L0_attn_ln2_b) + _L0_ffn_ref(xn, L0_ffn_Wr, L0_ffn_W1, L0_ffn_b1, L0_ffn_W2, L0_ffn_b2)
    return x

_drawn_inputs = setup_inputs


def setup_inputs(seed=0):
    import zlib

    import numpy as np

    out = dict(_drawn_inputs(seed))
    spreads = {'L0_attn_bq': (0.0, 2.0),
     'L0_attn_bk': (0.0, 2.0),
     'L0_attn_bv': (0.0, 0.472),
     'L0_attn_bo': (0.0, 0.1),
     'L0_attn_ln1_s': (1.0, 0.2),
     'L0_attn_ln1_b': (0.0, 0.1),
     'L0_attn_bf1': (0.0, 0.505),
     'L0_attn_bf2': (0.0, 0.1),
     'L0_attn_ln2_s': (1.0, 0.2),
     'L0_attn_ln2_b': (0.0, 0.1),
     'L0_ffn_b1': (0.0, 0.593),
     'L0_ffn_b2': (0.0, 0.407)}
    factors = {'L0_attn_Wq': 64.0, 'L0_attn_Wk': 8.0, 'L0_attn_Wv': 4.425, 'L0_attn_Wo': 3.111}
    for name, (base, spread) in spreads.items():
        noise = np.random.default_rng([zlib.crc32(name.encode()), seed]).standard_normal(out[name].shape)
        drawn = base * np.exp(spread * noise) if base else spread * noise
        out[name] = jnp.asarray(drawn.astype(out[name].dtype))
    for name, factor in factors.items():
        out[name] = (out[name] * factor).astype(out[name].dtype)
    return out
```

```python
import concourse.bass as bass
from concourse import mybir
from contextlib import ExitStack

L, D, F, E = 8, 128, 512, 8
T, P = 4096, 128
SEQ_TILES = 4
TS = 512
TILES = T // TS
STEPS = L * TILES
TT = T // P
MT = TT + E - 1
MTP = MT + 1
FC = F // P
EPS_LN, EPS_IN, EPS_Z = 1e-6, 1e-5, 1e-6
CQ, CK, CV, CO, CF1, CF2, CP = 0, 128, 256, 384, 512, 1024, 1536
BQ, BK, BV, BO, S1C, B1C, BF2, S2C, B2C, BF1 = range(10)
WCOLS = CP + 9 + FC
MCOLS = 2 * F + FC


def build(nc, x, wpack, wr, mpack, b2, out):
    f32, bf16, i32, u32 = mybir.dt.float32, mybir.dt.bfloat16, mybir.dt.int32, mybir.dt.uint32
    ALU, ACT, AX = mybir.AluOpType, mybir.ActivationFunctionType, mybir.AxisListType
    ctx = ExitStack()
    with ctx:
        def sb(name, shape, dt=f32):
            return ctx.enter_context(nc.sbuf_tensor(name, shape, dt))

        def sem(name):
            return ctx.enter_context(nc.semaphore(name))

        xs = nc.dram_tensor("moe_in", (MTP * P, D), f32, kind="Internal").ap()
        ys = nc.dram_tensor("moe_out", (MTP * P, D), f32, kind="Internal").ap()

        x0 = sb("x0", [P, TT, D])
        xn = sb("xn", [P, TT, D])
        xT = sb("xT", [P, T])
        w = sb("w", [P, 2, WCOLS])
        ident = sb("ident", [P, P])
        qz = sb("qz", [P, TILES, TS])
        mq = sb("mq", [P, 4, TS])
        kz = sb("kz", [P, 4, TS])
        mk = sb("mk", [P, 4, TS])
        vz = sb("vz", [P, 4, TS])
        sz = sb("sz", [P, 4, TS])
        ybuf = sb("ybuf", [P, 2, TS])
        nbuf = sb("nbuf", [P, 2, TS])
        x1 = sb("x1", [P, 2, TS])
        hb = sb("hb", [P, FC, TS])
        st = sb("st", [P, 2, 4, 6])
        ag = sb("ag", [P, 2, 4, 2])
        ve = sb("ve", [P, 2, 4])
        rstd = sb("rstd", [P, 2, 4])
        mhalf = sb("mhalf", [P, TT])
        kp = sb("kp", [P, TILES])
        kvp = sb("kvp", [P, TILES])
        ks = sb("ks", [P, 2, 6])
        nwo = sb("nwo", [P, 2, D])
        bo2 = sb("bo2", [P, 2])
        one = sb("one", [P, 1])
        epst = sb("epst", [P, 4])
        st0 = sb("st0", [P, TT, 6])
        ag0 = sb("ag0", [P, TT, 2])
        rs0 = sb("rs0", [P, 2, TT])
        wrs = sb("wrs", [P, E])
        rmx = sb("rmx", [P, TT])
        rd = sb("rd", [P, TT, E])
        re = sb("re", [P, TT, E])
        cand = sb("cand", [P, TT, E])
        cmx = sb("cmx", [P, TT])
        oh = sb("oh", [P, TT, E])
        ohb = sb("ohb", [P, TT, E], bf16)
        w8 = sb("w8", [P, E])
        psm = sb("psm", [P, TT])
        pmax = sb("pmax", [P, TT])
        tri = sb("tri", [P, P], bf16)
        onesb = sb("onesb", [P, P], bf16)
        tot = sb("tot", [P, TT, E])
        cum = sb("cum", [P, TT, E])
        onest = sb("onest", [P, TT])
        ntf = sb("ntf", [P, 4, E])
        nti = sb("nti", [P, 2, E], i32)
        slf = sb("slf", [P, TT])
        slot = sb("slot", [P, TT], u32)
        tix = sb("tix", [1, MTP])
        exf = sb("exf", [1, MTP])
        exi = sb("exi", [1, MTP], i32)
        ones_r = sb("ones_r", [1, P])
        wm = sb("wm", [P, 2, MCOLS])
        b2r = sb("b2r", [1, 2, D])
        mx = sb("mx", [P, 2, D])
        mxT = sb("mxT", [P, 2, D])
        mh = sb("mh", [P, 2, FC, P])
        my = sb("my", [P, 2, D])
        res = sb("res", [P, 4, 4, D])
        zero = res[:, 0, :, :].rearrange("p a d -> p (a d)")

        B = [ctx.enter_context(nc.psum_tensor(f"bank{i}", [P, TS], f32)) for i in range(8)]
        QKV, OB, O2, TOK, FEAT, HB = B[0:2], B[2], B[3], B[4], B[5], B[6:8]

        in_x, in_w, in_r = [sem(f"in_x{i}") for i in range(4)], [sem(f"in_w{i}") for i in range(2)], sem("in_r")
        consts = sem("consts")
        st0_d, ag0_d, ve0_d, rs0_d, xn_d = sem("st0_d"), sem("ag0_d"), sem("ve0_d"), sem("rs0_d"), sem("xn_d")
        xn_T, xT_d, logits_d, rchain, rexp = sem("xn_T"), sem("xT_d"), sem("logits_d"), sem("rchain"), sem("rexp")
        rdiff, onehot_d, counts_d, slots_d, expid_d = sem("rdiff"), sem("onehot_d"), sem("counts_d"), sem("slots_d"), sem("expid_d")
        zeroed, scattered, gathered = sem("zeroed"), sem("scattered"), sem("gathered")
        m_w = [sem(f"m_w{i}") for i in range(2)]
        m_T, m_xT, m_f1, m_h, m_f2, m_y, m_st = sem("m_T"), sem("m_xT"), sem("m_f1"), sem("m_h"), sem("m_f2"), sem("m_y"), [sem("m_st0"), sem("m_st1")]
        qkv_mm, qkv_ev, min_d, exp_d = sem("qkv_mm"), sem("qkv_ev"), sem("min_d"), sem("exp_d")
        K_d, KV_d, Q_d, cchain, coef_d, nwo_d, bo_mm, bo_d = (sem(n) for n in
            ("K_d", "KV_d", "Q_d", "cchain", "coef_d", "nwo_d", "bo_mm", "bo_d"))
        ln_d, s_d, eq_d = sem("ln_d"), sem("s_d"), sem("eq_d")
        o_mm, o_gelu, h_mm, h_gelu, f2_mm, f2_gelu = (sem(n) for n in ("o_mm", "o_gelu", "h_mm", "h_gelu", "f2_mm", "f2_gelu"))
        y_d, tok_d, bn_d, ag_d, ve_d, rs_d, nrm_d, feat_d, xo_d = ([sem(f"{n}{i}") for i in (1, 2)] for n in
            ("y_d", "tok_d", "bn_d", "ag_d", "ve_d", "rs_d", "nrm_d", "feat_d", "xo_d"))
        fin_T, fin_r1, fin_r2, fin_st = sem("fin_T"), sem("fin_r1"), sem("fin_r2"), [sem(f"fin_st{i}") for i in range(4)]

        block = ctx.enter_context(nc.Block())

        LOOP = range(2, 50)

        def steps(eng, step):
            for j in range(-6, LOOP.start):
                step(j, lambda k: 0)
            with eng.Fori(0, len(LOOP) // 16, 1) as turn:
                scaled = {k: eng.snap(turn * int(16 * k)) for k in (0.25, 1, 1.25, 2, 3, 4)}
                n = scaled.get
                for j in range(LOOP.start, LOOP.start + 16):
                    step(j, n)
            for j in range(LOOP.stop, STEPS + 2):
                step(j, lambda k: 0)

        def ok(i):
            return 0 <= i < STEPS

        def tile_of(i):
            return slice(i % TILES * TS, (i % TILES + 1) * TS)

        def lay(i):
            return i // TILES % 2

        def vec(i, c):
            return w[:, lay(i), CP + c:CP + c + 1]

        def seq(i):
            return i // SEQ_TILES % 2

        def nseq(i, n):
            return n(0.25) + i // SEQ_TILES + 1

        @block.sync
        def _(eng):
            for c in range(4):
                eng.dma_start(x0[:, 8 * c:8 * c + 8, :],
                              x[c * 1024:(c + 1) * 1024, :].rearrange("(a p) d -> p a d", p=P)).then_inc(in_x[c], 16)
            eng.dma_start(wrs[:, :], wr).then_inc(in_r, 16)
            for m in range(2):
                eng.dma_start(w[:, m, :], wpack[m, :, :]).then_inc(in_w[m], 16)
            eng.wait_ge(consts, 1)
            xz = xs.rearrange("(p a) d -> p (a d)", p=P)
            for c in range(MTP * D // TS):
                eng.dma_start(xz[:, c * TS:(c + 1) * TS], zero).then_inc(zeroed, 16)
            eng.wait_ge(expid_d, 1)
            eng.wait_ge(scattered, 16 * TT)

            def expert_tile(n, i, k):
                ex = eng.value_load(exi[0:1, bass.ds(i, 1)] if not isinstance(i, int) else exi[0:1, i:i + 1], min_val=0, max_val=E - 1)
                eng.dma_start(wm[:, n % 2, :], mpack[bass.ds(ex, 1), :, :].rearrange("e p c -> p (e c)")).then_inc(m_w[n % 2], 16)
                eng.dma_start(b2r[0:1, n % 2, :], b2[bass.ds(ex, 1), :]).then_inc(m_w[n % 2], 16)
                eng.dma_start(mx[:, n % 2, :], xs[bass.ds(k, P), :] if not isinstance(k, int) else xs[k:k + P, :]).then_inc(m_w[n % 2], 16)
            expert_tile(0, 0, 0)
            expert_tile(1, 1, P)
            with eng.Fori(0, MTP // 2 - 1, 1) as b:
                for n in range(2):
                    eng.wait_ge(m_f2, b * 2 + (n + 1))
                    expert_tile(n, b * 2 + (n + 2), b * (2 * P) + (n + 2) * P)
                    eng.wait_ge(m_y, b * 2 + (n + 1))
                    eng.dma_start(ys[bass.ds(b * (2 * P) + n * P, P), :], my[:, n % 2, :]).then_inc(m_st[n % 2], 16)
            for n in range(MTP - 2, MTP):
                eng.wait_ge(m_y, n + 1)
                eng.dma_start(ys[n * P:(n + 1) * P, :], my[:, n % 2, :]).then_inc(m_st[n % 2], 16)
            with eng.Fori(0, L // 2 - 1, 1) as b:
                for m in range(2):
                    eng.wait_ge(xo_d[1], b * (2 * TILES) + TILES * (m + 1))
                    eng.dma_start(w[:, m, :], wpack[bass.ds(b * 2 + (m + 2), 1), :, :].rearrange("l p c -> p (l c)")).then_inc(in_w[m], 16)
            ov = out.rearrange("(g a p) d -> g p a d", p=P, a=4)
            for g in range(TILES):
                eng.wait_ge(fin_r2, 4 * (g + 1))
                eng.dma_start(ov[g], res[:, g % 4, :, :]).then_inc(fin_st[g % 4], 16)
            for g in range(4):
                eng.wait_ge(fin_st[g], 16 * TILES // 4)

        @block.gpsimd
        def _(eng):
            eng.memset(zero, 0.0).then_inc(consts, 1)
            eng.memset(ident[:, :], 0.0).then_inc(consts, 1)
            eng.memset(mhalf[:, :], -0.5).then_inc(consts, 1)
            eng.memset(epst[:, :], EPS_LN).then_inc(consts, 1)
            eng.memset(one[:, :], 1.0).then_inc(consts, 1)
            eng.memset(onesb[:, :], 1.0).then_inc(consts, 1)
            eng.memset(onest[:, :], 1.0).then_inc(consts, 1)
            eng.memset(ones_r[:, :], 1.0).then_inc(consts, 1)
            eng.iota(w8[:, :], [[-1, E]], base=E, channel_multiplier=0, allow_small_or_imprecise_dtypes=True).then_inc(consts, 1)
            eng.iota(tix[:, :], [[1, MTP]], base=0, channel_multiplier=0, allow_small_or_imprecise_dtypes=True).then_inc(consts, 1)
            eng.wait_ge(consts, 10)
            eng.affine_select(out=ident[:, :], in_=ident[:, :], compare_op=ALU.not_equal, fill=1.0,
                              base=0, pattern=[[-1, P]], channel_multiplier=1).then_inc(consts, 1)
            eng.affine_select(out=tri[:, :], in_=onesb[:, :], compare_op=ALU.is_gt, fill=0.0,
                              base=0, pattern=[[1, P]], channel_multiplier=-1).then_inc(consts, 1)
            eng.wait_ge(ag0_d, 1)
            eng.tensor_scalar(rs0[:, 0, :], ag0[:, :, 1], EPS_IN, 1.0, ALU.add, ALU.mult).then_inc(ve0_d, 1)
            eng.wait_ge(ve0_d, 1)
            eng.tensor_tensor(out=rs0[:, 1, :], in0=rs0[:, 0, :], in1=mhalf[:, :], op=ALU.pow).then_inc(rs0_d, 1)
            eng.wait_ge(slots_d, 1)
            eng.wait_ge(zeroed, 16 * (MTP * D // TS))
            for t in range(TT):
                eng.indirect_dma_start(xs, bass.IndirectOffsetOnAxis(ap=slot[:, t:t + 1], axis=0),
                                       xn[:, t, :], None).then_inc(scattered, 16)
            eng.wait_ge(m_st[0], 16 * (MTP // 2))
            eng.wait_ge(m_st[1], 16 * (MTP // 2))
            for t in range(TT):
                eng.indirect_dma_start(xn[:, t, :], None, ys,
                                       bass.IndirectOffsetOnAxis(ap=slot[:, t:t + 1], axis=0)).then_inc(gathered, 16)

            def norm_root(g, i, n):
                eng.wait_ge(ag_d[i], n(1) + g + 1)
                eng.tensor_tensor(out=ve[:, i, :], in0=ag[:, i, :, 1], in1=epst[:, :], op=ALU.add).then_inc(ve_d[i], 1)
                eng.wait_ge(ve_d[i], n(1) + g + 1)
                eng.tensor_tensor(out=rstd[:, i, :], in0=ve[:, i, :], in1=mhalf[:, 0:4], op=ALU.pow).then_inc(rs_d[i], 1)

            def step(j, n):
                if ok(j):
                    norm_root(j, 0, n)
                if ok(j - 1):
                    norm_root(j - 1, 1, n)
            steps(eng, step)

        @block.scalar
        def _(eng):
            for g in range(TILES):
                eng.wait_ge(xn_T, 4 * (g + 1))
                eng.activation(xT[:, g * TS:(g + 1) * TS], B[g % 2][:, :], ACT.Copy).then_inc(xT_d, 1)
            eng.wait_ge(rdiff, 1)
            eng.activation(re[:, :, :].rearrange("p t e -> p (t e)"), rd[:, :, :].rearrange("p t e -> p (t e)"), ACT.Exp).then_inc(rexp, 1)

            def expert_gelus(n, b):
                eng.wait_ge(m_f1, b + n + 1)
                for f in range(FC):
                    eng.activation(mh[:, n % 2, f, :], B[2 + n % 2][:, f * P:(f + 1) * P], ACT.Gelu,
                                   bias=wm[:, n % 2, 2 * F + f:2 * F + f + 1]).then_inc(m_h, 1)
            with eng.Fori(0, MTP, 2) as b:
                for n in range(2):
                    expert_gelus(n, b)

            def step(j, n):
                if ok(j):
                    eng.wait_ge(o_mm, n(1) + j + 1)
                    eng.activation(OB[:, :], OB[:, :], ACT.Gelu_apprx_tanh, bias=bo2[:, seq(j):seq(j) + 1]).then_inc(o_gelu, 1)
                if ok(j - 1):
                    for f in range(FC):
                        eng.wait_ge(h_mm, n(4) + 4 * (j - 1) + f + 1)
                        eng.activation(hb[:, f, :], HB[f % 2][:, :], ACT.Gelu_apprx_tanh, bias=vec(j - 1, BF1 + f)).then_inc(h_gelu, 1)
                if ok(j - 2):
                    eng.wait_ge(feat_d[1], n(1) + j - 1)
                    eng.activation(xT[:, tile_of(j - 2)], FEAT[:, :], ACT.Identity, scale=vec(j - 2, S2C), bias=vec(j - 2, B2C)).then_inc(xo_d[1], 1)
                if j % 2:
                    window(j, n)
                if ok(j - 1):
                    eng.wait_ge(f2_mm, n(1) + j)
                    eng.activation(O2[:, :], O2[:, :], ACT.Gelu_apprx_tanh, bias=vec(j - 1, BF2)).then_inc(f2_gelu, 1)
                if ok(j):
                    eng.wait_ge(feat_d[0], n(1) + j + 1)
                    eng.activation(x1[:, j % 2, :], FEAT[:, :], ACT.Identity, scale=vec(j, S1C), bias=vec(j, B1C)).then_inc(xo_d[0], 1)
                a = j + 6
                if ok(a):
                    if a >= 4:
                        eng.wait_ge(KV_d, n(1) + a - 3)
                        eng.wait_ge(Q_d, n(1) + a - 3)
                    for c, (dst, b) in enumerate(((kz[:, a % 4, :], BK), (qz[:, a % TILES, :], BQ), (vz[:, a % 4, :], BV))):
                        eng.wait_ge(qkv_mm, n(3) + 3 * a + c + 1)
                        eng.activation(dst, QKV[(3 * a + c) % 2][:, :], ACT.Identity, bias=vec(a, b)).then_inc(qkv_ev, 1)

            def window(j, n):
                pair = [a for a in (j + 4, j + 5) if ok(a)]
                sp = [g for g in (j + 1, j + 2) if ok(g)]
                if pair or sp:
                    nc.scalar.preload_act_table_set("natural_log_exp_and_others")
                for a in pair:
                    eng.wait_ge(min_d, n(2) + 2 * a + 2)
                    eng.activation(mk[:, a % 4, :], mk[:, a % 4, :], ACT.Exp).then_inc(exp_d, 1)
                    eng.activation(mq[:, a % 4, :], mq[:, a % 4, :], ACT.Exp).then_inc(exp_d, 1)
                for g in sp:
                    eng.wait_ge(Q_d, n(1) + g + 1)
                    if g % SEQ_TILES == 0:
                        eng.wait_ge(coef_d, nseq(g, n))
                    eng.activation(sz[:, g % 4, :], qz[:, g % TILES, :], ACT.Ln, scale=ks[:, seq(g), 2:3], bias=one[:, 0:1]).then_inc(ln_d, 1)
                for g in sp:
                    eng.wait_ge(ln_d, n(1) + g + 1)
                    eng.activation(sz[:, g % 4, :], sz[:, g % 4, :], ACT.Exp, scale=-1.0).then_inc(s_d, 1)
                if pair or sp:
                    nc.scalar.preload_act_table_set("gelu_apprx_tanh_and_others")
            steps(eng, step)

        @block.vector
        def _(eng):
            for t in range(TT):
                eng.wait_ge(in_x[t // 8], 16)
                eng.bn_stats(st0[:, t, :], x0[:, t, :]).then_inc(st0_d, 1)
            for t in range(TT):
                eng.wait_ge(st0_d, TT)
                last = eng.bn_aggr(ag0[:, t, :], st0[:, t, :])
            last.then_inc(ag0_d, 1)
            eng.wait_ge(rs0_d, 1)
            for t in range(TT):
                eng.tensor_scalar(xn[:, t, :], x0[:, t, :], ag0[:, t, 0:1], rs0[:, 1, t:t + 1],
                                  ALU.subtract, ALU.mult).then_inc(xn_d, 1)
            chain = [0]

            def link(ins):
                chain[0] += 1
                ins.then_inc(rchain, 1)
                eng.wait_ge(rchain, chain[0])
            lg = B[2][:, 0:TT * E].rearrange("p (t e) -> p t e", e=E)
            eng.wait_ge(logits_d, 1)
            link(eng.tensor_reduce(rmx[:, :], lg, AX.X, ALU.max))
            eng.tensor_tensor(out=rd[:, :, :], in0=lg, in1=rmx[:, :].unsqueeze(2).broadcast_to([P, TT, E]), op=ALU.subtract).then_inc(rdiff, 1)
            eng.wait_ge(rdiff, 1)
            link(eng.tensor_scalar(cand[:, :, :], rd[:, :, :], 0.0, None, ALU.is_ge))
            link(eng.tensor_tensor(out=cand[:, :, :], in0=cand[:, :, :], in1=w8[:, :].unsqueeze(1).broadcast_to([P, TT, E]), op=ALU.mult))
            link(eng.tensor_reduce(cmx[:, :], cand[:, :, :], AX.X, ALU.max))
            link(eng.tensor_tensor(out=oh[:, :, :], in0=cand[:, :, :], in1=cmx[:, :].unsqueeze(2).broadcast_to([P, TT, E]), op=ALU.is_equal))
            eng.tensor_copy(ohb[:, :, :], oh[:, :, :]).then_inc(onehot_d, 1)
            eng.wait_ge(rexp, 1)
            link(eng.tensor_reduce(psm[:, :], re[:, :, :], AX.X, ALU.add))
            link(eng.reciprocal(pmax[:, :], psm[:, :]))
            eng.wait_ge(counts_d, 1)
            rank = B[4][:, 0:TT * E].rearrange("p (t e) -> p t e", e=E)
            link(eng.tensor_copy(tot[:, :, :], B[3][:, 0:TT * E].rearrange("p (t e) -> p t e", e=E)))
            for e in range(E):
                last = eng.tensor_tensor_scan(cum[:, :, e], onest[:, :], tot[:, :, e], 0.0, ALU.mult, ALU.add)
            link(last)
            link(eng.tensor_scalar(ntf[:, 0, :], cum[:, TT - 1, :], float(P - 1), None, ALU.add))
            link(eng.tensor_copy(nti[:, 0, :], ntf[:, 0, :]))
            link(eng.tensor_scalar(nti[:, 1, :], nti[:, 0, :], 7, None, ALU.logical_shift_right))
            link(eng.tensor_copy(ntf[:, 1, :], nti[:, 1, :]))
            link(eng.tensor_tensor_scan(ntf[:, 2, :], onest[:, 0:E], ntf[:, 1, :], 0.0, ALU.mult, ALU.add))
            link(eng.tensor_tensor(out=ntf[:, 3, :], in0=ntf[:, 2, :], in1=ntf[:, 1, :], op=ALU.subtract))
            link(eng.tensor_tensor(out=cum[:, :, :], in0=cum[:, :, :], in1=tot[:, :, :], op=ALU.subtract))
            link(eng.tensor_tensor(out=cum[:, :, :], in0=rank, in1=cum[:, :, :], op=ALU.add))
            link(eng.scalar_tensor_tensor(out=cum[:, :, :], in0=ntf[:, 3, :].unsqueeze(1).broadcast_to([P, TT, E]), scalar=float(P),
                                          in1=cum[:, :, :], op0=ALU.mult, op1=ALU.add))
            link(eng.tensor_tensor(out=cum[:, :, :], in0=cum[:, :, :], in1=oh[:, :, :], op=ALU.mult))
            link(eng.tensor_reduce(slf[:, :], cum[:, :, :], AX.X, ALU.add))
            eng.tensor_copy(slot[:, :], slf[:, :]).then_inc(slots_d, 1)
            link(eng.tensor_scalar(exf[:, :], tix[:, :], 0.0, -1.0, ALU.mult, ALU.add))
            for e in range(E):
                link(eng.scalar_tensor_tensor(out=exf[:, :], in0=tix[:, :], scalar=ntf[0:1, 3, e:e + 1],
                                              in1=exf[:, :], op0=ALU.is_ge, op1=ALU.add))
            eng.tensor_copy(exi[:, :], exf[:, :]).then_inc(expid_d, 1)

            def expert_copies(n, b, first):
                eng.wait_ge(m_T, b + n + 1)
                eng.tensor_copy(mxT[:, n % 2, :], B[n % 2][:, 0:P]).then_inc(m_xT, 1)
                eng.wait_ge(m_f2, b + n + 1)
                if not first:
                    eng.wait_ge(m_st[n % 2], (b * 8 if not isinstance(b, int) else 8 * b) + (n // 2) * 16)
                eng.tensor_copy(my[:, n % 2, :], B[4 + n % 2][:, 0:D]).then_inc(m_y, 1)
            expert_copies(0, 0, True)
            expert_copies(1, 0, True)
            with eng.Fori(0, MTP - 2, 2) as b:
                for n in range(2, 4):
                    expert_copies(n, b, False)

            def add(g, i, n):
                if i == 0:
                    eng.wait_ge(o_gelu, n(1) + g + 1)
                    eng.tensor_tensor(out=ybuf[:, 0, :], in0=OB[:, :], in1=xT[:, tile_of(g)], op=ALU.add).then_inc(y_d[0], 1)
                else:
                    eng.wait_ge(f2_gelu, n(1) + g + 1)
                    eng.tensor_tensor(out=ybuf[:, 1, :], in0=O2[:, :], in1=x1[:, g % 2, :], op=ALU.add).then_inc(y_d[1], 1)

            def norm(g, i, n):
                eng.wait_ge(tok_d[i], n(1) + g + 1)
                for c in range(4):
                    last = eng.bn_stats(st[:, i, c, :], TOK[:, c * P:(c + 1) * P])
                last.then_inc(bn_d[i], 1)
                eng.wait_ge(in_x[0], 16)
                eng.wait_ge(bn_d[i], n(1) + g + 1)
                for c in range(4):
                    last = eng.bn_aggr(ag[:, i, c, :], st[:, i, c, :])
                last.then_inc(ag_d[i], 1)
                eng.wait_ge(rs_d[i], n(1) + g + 1)
                for c in range(4):
                    last = eng.tensor_scalar(nbuf[:, i, c * P:(c + 1) * P], TOK[:, c * P:(c + 1) * P], ag[:, i, c, 0:1],
                                             rstd[:, i, c:c + 1], ALU.subtract, ALU.mult)
                last.then_inc(nrm_d[i], 1)

            def sums(a, n):
                eng.wait_ge(exp_d, n(2) + 2 * a + 2)
                eng.scalar_tensor_tensor(out=mk[:, a % 4, :], in0=kz[:, a % 4, :], scalar=1.0, in1=mk[:, a % 4, :],
                                         op0=ALU.add, op1=ALU.max, accum_out=kp[:, a % TILES:a % TILES + 1]).then_inc(K_d, 1)
                eng.tensor_scalar(mq[:, a % 4, :], mq[:, a % 4, :], -1.0, 1.0, ALU.add, ALU.add).then_inc(eq_d, 1)
                eng.wait_ge(eq_d, n(1) + a + 1)
                eng.scalar_tensor_tensor(out=qz[:, a % TILES, :], in0=qz[:, a % TILES, :], scalar=1.0, in1=mq[:, a % 4, :],
                                         op0=ALU.add, op1=ALU.max).then_inc(Q_d, 1)
                eng.wait_ge(K_d, n(1) + a + 1)
                eng.wait_ge(qkv_ev, n(3) + 3 * a + 3)
                eng.scalar_tensor_tensor(out=vz[:, a % 4, :], in0=vz[:, a % 4, :], scalar=1.0, in1=mk[:, a % 4, :],
                                         op0=ALU.mult, op1=ALU.mult, accum_out=kvp[:, a % TILES:a % TILES + 1]).then_inc(KV_d, 1)

            def coefficients(a, n):
                s = seq(a)
                first = a % TILES - 3

                def nth(k):
                    return n(1.25) + 5 * (a // SEQ_TILES) + k
                eng.wait_ge(KV_d, n(1) + a + 1)
                eng.tensor_reduce(ks[:, s, 0:1], kp[:, first:first + 4], AX.X, ALU.add).then_inc(cchain, 1)
                eng.tensor_reduce(ks[:, s, 1:2], kvp[:, first:first + 4], AX.X, ALU.add).then_inc(cchain, 1)
                eng.wait_ge(cchain, nth(2))
                eng.tensor_scalar(ks[:, s, 2:3], ks[:, s, 0:1], 1.0 / EPS_Z, None, ALU.mult).then_inc(coef_d, 1)
                eng.tensor_scalar(ks[:, s, 3:4], ks[:, s, 0:1], 1e-30, None, ALU.max).then_inc(cchain, 1)
                eng.wait_ge(cchain, nth(3))
                eng.reciprocal(ks[:, s, 4:5], ks[:, s, 3:4]).then_inc(cchain, 1)
                eng.wait_ge(cchain, nth(4))
                eng.tensor_tensor(out=ks[:, s, 5:6], in0=ks[:, s, 1:2], in1=ks[:, s, 4:5], op=ALU.mult).then_inc(cchain, 1)
                eng.wait_ge(cchain, nth(5))
                eng.tensor_scalar(nwo[:, s, :], w[:, lay(a), CO:CO + D], ks[:, s, 5:6], -1.0, ALU.mult, ALU.mult).then_inc(nwo_d, 1)

            def step(j, n):
                if ok(j):
                    add(j, 0, n)
                    norm(j, 0, n)
                if j % 2:
                    for a in (j + 4, j + 5):
                        if ok(a):
                            sums(a, n)
                            if a % SEQ_TILES == 3:
                                coefficients(a, n)
                if ok(j - 1):
                    add(j - 1, 1, n)
                g = j + 1
                if ok(g) and g % SEQ_TILES == 0:
                    eng.wait_ge(bo_mm, nseq(g, n))
                    eng.tensor_scalar(bo2[:, seq(g):seq(g) + 1], OB[:, 0:1], vec(g, BO), None, ALU.add).then_inc(bo_d, 1)
                a = j + 6
                if ok(a):
                    eng.wait_ge(qkv_ev, n(3) + 3 * a + 1)
                    eng.tensor_scalar(mk[:, a % 4, :], kz[:, a % 4, :], 0.0, None, ALU.min).then_inc(min_d, 1)
                    eng.wait_ge(qkv_ev, n(3) + 3 * a + 2)
                    eng.tensor_scalar(mq[:, a % 4, :], qz[:, a % TILES, :], 0.0, None, ALU.min).then_inc(min_d, 1)
                if ok(j - 1):
                    norm(j - 1, 1, n)
            steps(eng, step)
            for g in range(TILES):
                eng.wait_ge(fin_T, 4 * (g + 1))
                if g >= 4:
                    eng.wait_ge(fin_st[g % 4], 16)
                eng.tensor_tensor(out=res[:, g % 4, :, :], in0=B[g % 2][:, :].rearrange("p (a d) -> p a d", a=4),
                                  in1=x0[:, 4 * g:4 * g + 4, :], op=ALU.add).then_inc(fin_r1, 1)
                eng.wait_ge(fin_r1, g + 1)
                if g == 0:
                    eng.wait_ge(gathered, 16 * TT)
                for c in range(4):
                    t = 4 * g + c
                    eng.scalar_tensor_tensor(out=res[:, g % 4, c, :], in0=xn[:, t, :], scalar=pmax[:, t:t + 1],
                                             in1=res[:, g % 4, c, :], op0=ALU.mult, op1=ALU.add).then_inc(fin_r2, 1)

        @block.tensor
        def _(eng):
            eng.wait_ge(consts, 12)
            for g in range(TILES):
                eng.wait_ge(xn_d, 4 * (g + 1))
                if g >= 2:
                    eng.wait_ge(xT_d, g - 1)
                for c in range(4):
                    eng.transpose(B[g % 2][:, c * P:(c + 1) * P], xn[:, 4 * g + c, :], ident[:, :]).then_inc(xn_T, 1)
            eng.wait_ge(in_r, 16)
            for t in range(TT):
                eng.wait_ge(xT_d, t // 4 + 1)
                last = eng.matmul(B[2][:, t * E:(t + 1) * E], xT[:, t * P:(t + 1) * P], wrs[:, :], start=True, stop=True)
            last.then_inc(logits_d, 1)
            eng.wait_ge(onehot_d, 1)
            ohv = ohb[:, :, :].rearrange("p t e -> p (t e)")
            eng.matmul(B[3][:, 0:TT * E], onesb[:, :], ohv, start=True, stop=True)
            eng.matmul(B[4][:, 0:TT * E], tri[:, :], ohv, start=True, stop=True).then_inc(counts_d, 1)
            eng.wait_ge(expid_d, 1)

            def expert_products(n, b, b4, b24, first):
                eng.wait_ge(m_w[n % 2], b24 + 48 * (n // 2) + 48)
                eng.transpose(B[n % 2][:, 0:P], mx[:, n % 2, :], ident[:, :]).then_inc(m_T, 1)
                eng.wait_ge(m_xT, b + n + 1)
                if not first:
                    eng.wait_ge(m_h, b4 + 4 * (n - 1))
                for f in range(FC):
                    last = eng.matmul(B[2 + n % 2][:, f * P:(f + 1) * P], wm[:, n % 2, f * P:(f + 1) * P], mxT[:, n % 2, :],
                                      start=True, stop=True)
                last.then_inc(m_f1, 1)
                if not first:
                    eng.wait_ge(m_y, b + n - 1)
                for f in range(FC):
                    eng.wait_ge(m_h, b4 + 4 * n + f + 1)
                    eng.matmul(B[4 + n % 2][:, 0:D], mh[:, n % 2, f, :], wm[:, n % 2, F + f * D:F + (f + 1) * D],
                               start=(f == 0), stop=False)
                eng.matmul(B[4 + n % 2][:, 0:D], ones_r[:, :], b2r[:, n % 2, :], start=False, stop=True).then_inc(m_f2, 1)
            expert_products(0, 0, 0, 0, True)
            expert_products(1, 0, 0, 0, True)
            with eng.Fori(0, MTP - 2, 2) as b:
                b4, b24 = eng.snap(b * 4), eng.snap(b * 24)
                for n in range(2, 4):
                    expert_products(n, b, b4, b24, False)

            def W(i, c, width=D):
                return w[:, lay(i), c:c + width]

            def to_tokens(g, i, n):
                eng.wait_ge(y_d[i], n(1) + g + 1)
                if i == 0 and g >= 2:
                    eng.wait_ge(nrm_d[1], n(1) + g - 1)
                if i == 1 and g + 1 < STEPS:
                    eng.wait_ge(nrm_d[0], n(1) + g + 2)
                for c in range(4):
                    last = eng.transpose(TOK[:, c * P:(c + 1) * P], ybuf[:, i, c * P:(c + 1) * P], ident[:, :])
                last.then_inc(tok_d[i], 1)

            def to_features(g, i, n):
                eng.wait_ge(nrm_d[i], n(1) + g + 1)
                if i == 0 and g >= 2:
                    eng.wait_ge(xo_d[1], n(1) + g - 1)
                if i == 1:
                    eng.wait_ge(xo_d[0], n(1) + (g + 2 if g + 1 < STEPS else g + 1))
                for c in range(4):
                    last = eng.transpose(FEAT[:, c * P:(c + 1) * P], nbuf[:, i, c * P:(c + 1) * P], ident[:, :])
                last.then_inc(feat_d[i], 1)

            def project(a, c, n):
                if a % TILES == 0 and c == 0:
                    eng.wait_ge(in_w[lay(a)], n(1) + a // (2 * TILES) * 16 + 16)
                if 3 * a + c >= 2:
                    eng.wait_ge(qkv_ev, n(3) + 3 * a + c - 1)
                eng.matmul(QKV[(3 * a + c) % 2][:, :], W(a, (CK, CQ, CV)[c]), xT[:, tile_of(a)], start=True, stop=True).then_inc(qkv_mm, 1)

            def step(j, n):
                if ok(j):
                    eng.wait_ge(s_d, n(1) + j + 1)
                    if j % SEQ_TILES == 0:
                        eng.wait_ge(nwo_d, nseq(j, n))
                        eng.wait_ge(bo_d, nseq(j, n))
                    if j >= 1:
                        eng.wait_ge(y_d[0], n(1) + j)
                    eng.matmul(OB[:, :], nwo[:, seq(j), :], sz[:, j % 4, :], start=True, stop=True).then_inc(o_mm, 1)
                if ok(j - 1):
                    g = j - 1
                    eng.wait_ge(xo_d[0], n(1) + g + 1)
                    for f in range(FC):
                        if 4 * g + f >= 2:
                            eng.wait_ge(h_gelu, n(4) + 4 * g + f - 1)
                        eng.matmul(HB[f % 2][:, :], W(g, CF1 + f * P, P), x1[:, g % 2, :], start=True, stop=True).then_inc(h_mm, 1)
                if ok(j):
                    to_tokens(j, 0, n)
                if ok(j - 2):
                    to_features(j - 2, 1, n)
                if ok(j - 1):
                    if g >= 1:
                        eng.wait_ge(y_d[1], n(1) + g)
                    for f in range(FC):
                        eng.wait_ge(h_gelu, n(4) + 4 * g + f + 1)
                        last = eng.matmul(O2[:, :], W(g, CF2 + f * D), hb[:, f, :], start=(f == 0), stop=(f == FC - 1))
                    last.then_inc(f2_mm, 1)
                if ok(j):
                    to_features(j, 0, n)
                a = j + 6
                if ok(a):
                    if a >= TILES:
                        eng.wait_ge(xo_d[1], n(1) + a - TILES + 1)
                    project(a, 0, n)
                    project(a, 1, n)
                g = j + 1
                if ok(g) and g % SEQ_TILES == 0:
                    eng.wait_ge(nwo_d, nseq(g, n))
                    if j >= 0:
                        eng.wait_ge(y_d[0], n(1) + j + 1)
                    eng.matmul(OB[:, 0:1], W(g, CO), ks[:, seq(g), 5:6], start=True, stop=True).then_inc(bo_mm, 1)
                if ok(j - 1):
                    to_tokens(j - 1, 1, n)
                if ok(a):
                    project(a, 2, n)
            steps(eng, step)
            for g in range(TILES):
                eng.wait_ge(xo_d[1], STEPS - TILES + g + 1)
                if g >= 2:
                    eng.wait_ge(fin_r1, g - 1)
                for c in range(4):
                    eng.transpose(B[g % 2][:, c * P:(c + 1) * P], xT[:, g * TS + c * P:g * TS + (c + 1) * P], ident[:, :]).then_inc(fin_T, 1)


def kernel(**inputs):
    import numpy as np
    import concourse.bacc as bacc
    from concourse import mybir as mb
    from concourse.bass_utils import run_bass_kernel_spmd as run

    a = {k: np.asarray(v) for k, v in inputs.items()}
    at = {k[8:]: v for k, v in a.items() if k.startswith("L0_attn_")}
    ff = {k[7:]: v for k, v in a.items() if k.startswith("L0_ffn_")}
    vecs = [at[n][:, :, None] for n in ("bq", "bk", "bv", "bo", "ln1_s", "ln1_b", "bf2", "ln2_s", "ln2_b")]
    wf2 = at["Wf2"].reshape(L, FC, P, D).transpose(0, 2, 1, 3).reshape(L, P, FC * D)
    bf1 = at["bf1"].reshape(L, FC, P).transpose(0, 2, 1)
    wpack = np.ascontiguousarray(np.concatenate([at["Wq"], at["Wk"], at["Wv"], at["Wo"], at["Wf1"], wf2, *vecs, bf1], axis=2))
    w2 = ff["W2"].reshape(E, FC, P, D).transpose(0, 2, 1, 3).reshape(E, P, FC * D)
    mpack = np.ascontiguousarray(np.concatenate([ff["W1"], w2, ff["b1"].reshape(E, FC, P).transpose(0, 2, 1)], axis=2))
    arrays = {"x": np.ascontiguousarray(at["x"]).reshape(T, D), "wpack": wpack, "wr": np.ascontiguousarray(ff["Wr"]),
              "mpack": mpack, "b2": np.ascontiguousarray(ff["b2"])}
    nc = bacc.Bacc("TRN2", target_bir_lowering=False, num_devices=1)
    args = [nc.dram_tensor(n, v.shape, mb.dt.from_np(v.dtype), kind="ExternalInput").ap() for n, v in arrays.items()]
    o = nc.dram_tensor("out", (T, D), mb.dt.float32, kind="ExternalOutput").ap()
    build(nc, *args, o)
    r = run(nc, [arrays], core_ids=[0])
    return r.results[0]["out"].reshape(2, T // 2, D)
```

```python
import concourse.bass as bass
from concourse import mybir
from contextlib import ExitStack

L, D, F, E = 8, 128, 512, 8
T, P = 4096, 128
SEQ_TILES = 4
TS = 512
TILES = T // TS
STEPS = L * TILES
TT = T // P
MT = TT + E - 1
MTP = MT + 1
FC = F // P
EPS_LN, EPS_IN, EPS_Z = 1e-6, 1e-5, 1e-6
CQ, CK, CV, CF1 = 0, D, 2 * D, 3 * D
SCOLS = 3 * D + F
CO, CF2, CP = 0, D, D + F
BQ, BK, BV, BO, S1C, B1C, BF2, S2C, B2C, BF1 = range(10)
WCOLS = CP + 9 + FC
PAIRS = MTP // 2
MCOLS = 2 * F + FC


def build(nc, x, spack, wpack, wr, mpack, b2, out):
    f32, f32r, bf16, i32, u32 = mybir.dt.float32, mybir.dt.float32r, mybir.dt.bfloat16, mybir.dt.int32, mybir.dt.uint32
    ALU, ACT, AX = mybir.AluOpType, mybir.ActivationFunctionType, mybir.AxisListType
    ctx = ExitStack()
    with ctx:
        def sb(name, shape, dt=f32):
            return ctx.enter_context(nc.sbuf_tensor(name, shape, dt))

        def sem(name):
            return ctx.enter_context(nc.semaphore(name))

        xs = nc.dram_tensor("moe_in", (MTP * P, D), f32, kind="Internal").ap()
        ys = nc.dram_tensor("moe_out", (MTP * P, D), f32, kind="Internal").ap()

        x0 = sb("x0", [P, TT, D])
        xT = sb("xT", [P, T])
        w = sb("w", [P, 2, WCOLS])
        wst = sb("wst", [P, SCOLS])
        wh = sb("wh", [P, 2, SCOLS], f32r)
        wl = sb("wl", [P, 2, SCOLS], f32r)
        xh = sb("xh", [P, TS], f32r)
        xl = sb("xl", [P, TS], f32r)
        x1h = sb("x1h", [P, TS], f32r)
        x1l = sb("x1l", [P, TS], f32r)
        ident = sb("ident", [P, P])
        nil = sb("nil", [P, SCOLS])
        qz = sb("qz", [P, TILES, TS])
        mq = sb("mq", [P, 4, TS])
        kvz = sb("kvz", [P, 8, TS])
        kz, vz = kvz[:, 0:4, :], kvz[:, 4:8, :]
        xg = kvz[:, :, :].rearrange("p (t a) (b d) -> p (t a b) d", a=1, d=D)
        mk = sb("mk", [P, 4, TS])
        shx = sb("shx", [P, 8, TS])
        xn = shx[:, :, :].rearrange("p (t a) (b d) -> p (t a b) d", a=1, d=D)
        sz = sb("sz", [P, 4, TS])
        hb = shx[:, 4:8, :]
        ybuf = sb("ybuf", [P, 2, TS])
        nbuf = sb("nbuf", [P, 2, TS])
        x1 = sb("x1", [P, 2, TS])
        st = sb("st", [P, 2, 4, 6])
        ag = sb("ag", [P, 2, 4, 2])
        ve = sb("ve", [P, 2, 4])
        rstd = sb("rstd", [P, 2, 4])
        mhalf = sb("mhalf", [P, TT])
        kp = sb("kp", [P, TILES])
        kvp = sb("kvp", [P, TILES])
        ks = sb("ks", [P, 2, 6])
        nwo = sb("nwo", [P, 2, D])
        bo2 = sb("bo2", [P, 2])
        one = sb("one", [P, 1])
        epst = sb("epst", [P, 4])
        st0 = sb("st0", [P, TT, 6])
        ag0 = sb("ag0", [P, TT, 2])
        rs0 = sb("rs0", [P, 2, TT])
        wrs = sb("wrs", [P, E])
        rmx = sb("rmx", [P, TT])
        rd = sb("rd", [P, TT, E])
        re = sb("re", [P, TT, E])
        cand = sb("cand", [P, TT, E])
        cmx = sb("cmx", [P, TT])
        oh = sb("oh", [P, TT, E])
        ohb = sb("ohb", [P, TT, E], bf16)
        w8 = sb("w8", [P, E])
        psm = sb("psm", [P, TT])
        pmax = sb("pmax", [P, TT])
        tri = sb("tri", [P, P], bf16)
        onesb = sb("onesb", [P, P], bf16)
        tot = sb("tot", [P, TT, E])
        cum = sb("cum", [P, TT, E])
        onest = sb("onest", [P, TT])
        ntf = sb("ntf", [P, 4, E])
        nti = sb("nti", [P, 2, E], i32)
        slf = sb("slf", [P, TT])
        slot = sb("slot", [P, TT], u32)
        tix = sb("tix", [1, MTP])
        exf = sb("exf", [1, MTP])
        exi = sb("exi", [1, MTP], i32)
        ones_r = sb("ones_r", [1, P])
        wm = sb("wm", [P, 2, MCOLS])
        b2r = sb("b2r", [1, 2, D])
        mx = sb("mx", [P, 2, D])
        mxT = sb("mxT", [P, 2, D])
        mh = sb("mh", [P, 2, FC, P])
        my = sb("my", [P, 2, D])
        res = qz[:, 0:4, :].rearrange("p g (a d) -> p g a d", d=D)
        zero = nil[:, 0:TS]

        B = [ctx.enter_context(nc.psum_tensor(f"bank{i}", [P, TS], f32)) for i in range(8)]
        QKV, OB, O2, TOK, HB = B[0:2], B[2], B[3], B[4:6], B[6:8]

        in_x, in_w, in_r = [sem(f"in_x{i}") for i in range(4)], [sem(f"in_w{i}") for i in range(2)], sem("in_r")
        in_s, wh_d, wl_d, xh_d, xl_d, x1h_d, x1l_d = (sem(n) for n in ("in_s", "wh_d", "wl_d", "xh_d", "xl_d", "x1h_d", "x1l_d"))
        consts = sem("consts")
        st0_d, ag0_d, ve0_d, rs0_d, xn_d = sem("st0_d"), sem("ag0_d"), sem("ve0_d"), sem("rs0_d"), sem("xn_d")
        xn_T, xT_d, logits_d, rchain, rexp = sem("xn_T"), sem("xT_d"), sem("logits_d"), sem("rchain"), sem("rexp")
        rdiff, onehot_d, counts_d, slots_d, expid_d = sem("rdiff"), sem("onehot_d"), sem("counts_d"), sem("slots_d"), sem("expid_d")
        zeroed, scattered, gathered = sem("zeroed"), [sem(f"scattered{i}") for i in range(2)], sem("gathered")
        m_w = [sem(f"m_w{i}") for i in range(2)]
        m_T, m_xT, m_f1, m_h, m_f2, m_y, m_st = sem("m_T"), sem("m_xT"), sem("m_f1"), sem("m_h"), sem("m_f2"), sem("m_y"), sem("m_st")
        qkv_mm, qkv_ev, min_d, exp_k, exp_q = (sem(n) for n in ("qkv_mm", "qkv_ev", "min_d", "exp_k", "exp_q"))
        K_d, KV_d, Q_d, cchain, coef_d, nwo_d, bo_mm, bo_d = (sem(n) for n in
            ("K_d", "KV_d", "Q_d", "cchain", "coef_d", "nwo_d", "bo_mm", "bo_d"))
        ln_d, s_d, eq_d = sem("ln_d"), sem("s_d"), sem("eq_d")
        o_mm, o_gelu, h_mm, h_gelu, f2_mm, f2_gelu = (sem(n) for n in ("o_mm", "o_gelu", "h_mm", "h_gelu", "f2_mm", "f2_gelu"))
        y_d, tok_d, bn_d, ag_d, ve_d, rs_d, nrm_d, feat_d, xo_d = ([sem(f"{n}{i}") for i in (1, 2)] for n in
            ("y_d", "tok_d", "bn_d", "ag_d", "ve_d", "rs_d", "nrm_d", "feat_d", "xo_d"))
        fin_T, fin_r1, fin_r2, fin_st = sem("fin_T"), sem("fin_r1"), sem("fin_r2"), [sem(f"fin_st{i}") for i in range(4)]

        block = ctx.enter_context(nc.Block())

        LOOP = range(2, 50)
        PSTEPS = (2, 4, 6, 8, 12, 14)
        PTURN = len(PSTEPS)

        def steps(eng, step, first=-6):
            for j in range(first, LOOP.start):
                step(j, lambda k: 0)
            with eng.Fori(0, len(LOOP) // 16, 1) as turn:
                scaled = {k: eng.snap(turn * int(16 * k)) for k in (0.125, 0.25, PTURN / 16, 1, 1.25, 2, 3, 4, 6, 18)}
                n = scaled.get
                for j in range(LOOP.start, LOOP.start + 16):
                    step(j, n)
            for j in range(LOOP.stop, STEPS + 2):
                step(j, lambda k: 0)

        def ok(i):
            return 0 <= i < STEPS

        def pair(j):
            if j < LOOP.start:
                return None
            if j < LOOP.stop:
                k = (j - LOOP.start) % 16
                return PTURN * ((j - LOOP.start) // 16) + PSTEPS.index(k) if k in PSTEPS else None
            p = PTURN * (len(LOOP) // 16) + (j - LOOP.stop) // 2
            return p if j % 2 == 0 and p < PAIRS else None

        def by_vector(j):
            return j % 2 == 1 or pair(j) is not None

        def bank(a, c):
            return QKV[(3 * a + c) % 2][:, :]

        def tile_of(i):
            return slice(i % TILES * TS, (i % TILES + 1) * TS)

        def lay(i):
            return i // TILES % 2

        def vec(i, c):
            return w[:, lay(i), CP + c:CP + c + 1]

        def seq(i):
            return i // SEQ_TILES % 2

        def nseq(i, n):
            return n(0.25) + i // SEQ_TILES + 1

        def wait_input(eng, a, n):
            if a >= TILES:
                eng.wait_ge(xo_d[1], n(1) + a - TILES + 1)
            else:
                eng.wait_ge(xT_d, a + 1)
            if a >= 1:
                eng.wait_ge(qkv_mm, n(3) + 3 * a)

        def finished(j):
            return {61: (0, 1), 62: (2,), 63: (3, 4), 64: (5,), 65: (6,)}.get(j, ())

        @block.sync
        def _(eng):
            for c in range(4):
                eng.dma_start(x0[:, 8 * c:8 * c + 8, :],
                              x[c * 1024:(c + 1) * 1024, :].rearrange("(a p) d -> p a d", p=P)).then_inc(in_x[c], 16)
            eng.dma_start(wrs[:, :], wr).then_inc(in_r, 16)
            eng.dma_start(wst[:, :], spack[0, :, :]).then_inc(in_s, 16)
            for m in range(2):
                eng.dma_start(w[:, m, :], wpack[m, :, :]).then_inc(in_w[m], 16)
            eng.wait_ge(consts, 1)
            xz = xs.rearrange("(p a) d -> p (a d)", p=P)
            for c in range(MTP * D // TS):
                eng.dma_start(xz[:, c * TS:(c + 1) * TS], zero).then_inc(zeroed, 16)

            def split_weights(m):
                eng.wait_ge(wl_d, m)
                eng.dma_start(wst[:, :], spack[bass.ds(m, 1), :, :].rearrange("l p c -> p (l c)")).then_inc(in_s, 16)

            def load_experts(row):
                for i in range(2):
                    ex = eng.value_load(exi[0:1, bass.ds(row + i, 1)], min_val=0, max_val=E - 1)
                    eng.dma_start(wm[:, i, :], mpack[bass.ds(ex, 1), :, :].rearrange("e p c -> p (e c)")).then_inc(m_w[i], 16)
                    eng.dma_start(b2r[0:1, i, :], b2[bass.ds(ex, 1), :]).then_inc(m_w[i], 16)
                    eng.dma_start(mx[:, i, :], xs[bass.ds((row + i) * P, P), :]).then_inc(m_w[i], 16)

            def step(j, n):
                if j == 1:
                    eng.wait_ge(expid_d, 1)
                    for half in scattered:
                        eng.wait_ge(half, 16 * TT // 2)
                    load_experts(0)
                if j % TILES == TILES - 1 and 0 < (j + 9) // TILES < L:
                    split_weights(n(0.125) + (j + 9) // TILES)
                if (j + 7) % TILES == 0 and (j + 7) // TILES < L:
                    m = (j + 7) // TILES
                    if m >= 2:
                        eng.wait_ge(xo_d[1], n(1) + j - 1)
                        eng.dma_start(w[:, m % 2, :], wpack[bass.ds(n(0.125) + m, 1), :, :].rearrange("l p c -> p (l c)")).then_inc(in_w[m % 2], 16)
                p = pair(j)
                if p is not None:
                    eng.wait_ge(m_f2, n(PTURN / 16) + p + 1)
                    if p + 1 < PAIRS:
                        load_experts(n(PTURN / 16) * 2 + 2 * (p + 1))
                    eng.wait_ge(m_y, n(PTURN / 16) + p + 1)
                    eng.dma_start(ys[bass.ds((n(PTURN / 16) + p) * (2 * P), 2 * P), :].rearrange("(i p) d -> p i d", i=2), my[:, :, :]).then_inc(m_st, 16)
            steps(eng, step, first=-7)
            ov = out.rearrange("(g a p) d -> g p a d", p=P, a=4)
            for g in range(TILES):
                eng.wait_ge(fin_r2, 4 * (g + 1))
                eng.dma_start(ov[g], res[:, g % 4, :, :]).then_inc(fin_st[g % 4], 16)
            for g in range(4):
                eng.wait_ge(fin_st[g], 16 * TILES // 4)

        @block.gpsimd
        def _(eng):
            eng.memset(nil[:, :], 0.0).then_inc(consts, 1)
            eng.memset(ident[:, :], 0.0).then_inc(consts, 1)
            eng.memset(mhalf[:, :], -0.5).then_inc(consts, 1)
            eng.memset(epst[:, :], EPS_LN).then_inc(consts, 1)
            eng.memset(one[:, :], 1.0).then_inc(consts, 1)
            eng.memset(onesb[:, :], 1.0).then_inc(consts, 1)
            eng.memset(onest[:, :], 1.0).then_inc(consts, 1)
            eng.memset(ones_r[:, :], 1.0).then_inc(consts, 1)
            eng.iota(w8[:, :], [[-1, E]], base=E, channel_multiplier=0, allow_small_or_imprecise_dtypes=True).then_inc(consts, 1)
            eng.iota(tix[:, :], [[1, MTP]], base=0, channel_multiplier=0, allow_small_or_imprecise_dtypes=True).then_inc(consts, 1)
            eng.wait_ge(consts, 10)
            eng.affine_select(out=ident[:, :], in_=ident[:, :], compare_op=ALU.not_equal, fill=1.0,
                              base=0, pattern=[[-1, P]], channel_multiplier=1).then_inc(consts, 1)
            eng.affine_select(out=tri[:, :], in_=onesb[:, :], compare_op=ALU.is_gt, fill=0.0,
                              base=0, pattern=[[1, P]], channel_multiplier=-1).then_inc(consts, 1)
            def split_weights(a, n):
                eng.wait_ge(in_s, n(2) + 2 * a + 16)
                eng.tensor_tensor(out=wh[:, lay(a), :], in0=wst[:, :], in1=nil[:, :], op=ALU.add).then_inc(wh_d, 1)
                eng.wait_ge(wh_d, n(0.125) + a // TILES + 1)
                eng.tensor_tensor(out=wl[:, lay(a), :], in0=wst[:, :], in1=wh[:, lay(a), :].bitcast(f32), op=ALU.subtract).then_inc(wl_d, 1)

            for c in range(4):
                part = slice(8 * c, 8 * c + 8)
                eng.wait_ge(ag0_d, c + 1)
                eng.tensor_scalar(rs0[:, 0, part], ag0[:, part, 1], EPS_IN, 1.0, ALU.add, ALU.mult).then_inc(ve0_d, 1)
                eng.wait_ge(ve0_d, c + 1)
                eng.tensor_tensor(out=rs0[:, 1, part], in0=rs0[:, 0, part], in1=mhalf[:, part], op=ALU.pow).then_inc(rs0_d, 1)
            split_weights(0, lambda k: 0)

            SCATTER = {-3: (4,), -2: (5, 6), -1: (7, 0), 0: (1, 2), 1: (3,)}

            def scatter(first):
                for t in range(first, first + 4):
                    eng.indirect_dma_start(xs, bass.IndirectOffsetOnAxis(ap=slot[:, t:t + 1], axis=0),
                                           xn[:, t, :], None).then_inc(scattered[t // (TT // 2)], 16)

            def norm_root(g, i, n):
                eng.wait_ge(ag_d[i], n(1) + g + 1)
                eng.tensor_tensor(out=ve[:, i, :], in0=ag[:, i, :, 1], in1=epst[:, :], op=ALU.add).then_inc(ve_d[i], 1)
                eng.wait_ge(ve_d[i], n(1) + g + 1)
                eng.tensor_tensor(out=rstd[:, i, :], in0=ve[:, i, :], in1=mhalf[:, 0:4], op=ALU.pow).then_inc(rs_d[i], 1)

            def gather(j, part):
                if not 57 <= j < 61:
                    return
                if part[0] == 0:
                    eng.wait_ge(m_st, 16 * PAIRS)
                    eng.wait_ge(KV_d, j + 4)
                groups = (*range(4 * (j - 57), 4 * (j - 56)), *range(4 * (j - 53), 4 * (j - 52)))
                for t in (groups[i] for i in part):
                    eng.indirect_dma_start(xg[:, t, :], None, ys,
                                           bass.IndirectOffsetOnAxis(ap=slot[:, t:t + 1], axis=0)).then_inc(gathered, 16)

            def step(j, n):
                a = j + 6
                if ok(j - 2):
                    norm_root(j - 2, 1, n)
                if ok(j):
                    norm_root(j, 0, n)
                if j == -3:
                    eng.wait_ge(slots_d, 1)
                    eng.wait_ge(zeroed, 16 * (MTP * D // TS))
                for q in SCATTER.get(j, ())[1:]:
                    scatter(4 * q)
                gather(j, range(6))
                if ok(a):
                    eng.wait_ge(xh_d, n(1) + a + 1)
                    eng.tensor_tensor(out=xl[:, :], in0=xT[:, tile_of(a)], in1=xh[:, :].bitcast(f32), op=ALU.subtract).then_inc(xl_d, 1)
                if ok(j):
                    eng.wait_ge(x1h_d, n(1) + j + 1)
                    eng.tensor_tensor(out=x1l[:, :], in0=x1[:, j % 2, :], in1=x1h[:, :].bitcast(f32), op=ALU.subtract).then_inc(x1l_d, 1)
                for q in SCATTER.get(j, ())[:1]:
                    scatter(4 * q)
                gather(j, range(6, 8))
                if ok(a + 1) and (a + 1) % TILES == 0:
                    split_weights(a + 1, n)
            steps(eng, step)

        @block.scalar
        def _(eng):
            for g in range(TILES):
                eng.wait_ge(xn_T, 4 * (g + 1))
                eng.activation(xT[:, g * TS:(g + 1) * TS], B[g % 2][:, :], ACT.Copy).then_inc(xT_d, 1)

            def probabilities():
                eng.wait_ge(rdiff, 1)
                eng.activation(re[:, :, :].rearrange("p t e -> p (t e)"), rd[:, :, :].rearrange("p t e -> p (t e)"), ACT.Exp).then_inc(rexp, 1)

            def expert_gelus(p, n):
                nc.scalar.preload_act_table_set("gelu_and_others")
                for i in range(2):
                    eng.wait_ge(m_f1, n(PTURN / 16) * 2 + 2 * p + i + 1)
                    for f in range(FC):
                        last = eng.activation(mh[:, i, f, :], HB[i][:, f * P:(f + 1) * P], ACT.Gelu,
                                              bias=wm[:, i, 2 * F + f:2 * F + f + 1])
                    last.then_inc(m_h, 1)
                nc.scalar.preload_act_table_set("gelu_apprx_tanh_and_others")

            def step(j, n):
                if ok(j):
                    if j % SEQ_TILES == 0:
                        eng.wait_ge(bo_d, nseq(j, n))
                    eng.wait_ge(o_mm, n(1) + j + 1)
                    eng.activation(OB[:, :], OB[:, :], ACT.Gelu_apprx_tanh, bias=bo2[:, seq(j):seq(j) + 1]).then_inc(o_gelu, 1)
                v = j + 5
                if ok(v):
                    if v >= 4:
                        eng.wait_ge(KV_d, n(1) + v - 3)
                    eng.wait_ge(qkv_mm, n(3) + 3 * v + 3)
                    eng.wait_ge(qkv_ev, n(3) + 3 * v + 2)
                    eng.activation(vz[:, v % 4, :], QKV[(3 * v + 2) % 2][:, :], ACT.Identity, bias=vec(v, BV)).then_inc(qkv_ev, 1)
                if j == 1:
                    eng.wait_ge(scattered[1], 16 * TT // 2)
                if ok(j - 1):
                    for f in range(FC):
                        eng.wait_ge(h_mm, n(4) + 4 * (j - 1) + f + 1)
                        eng.activation(hb[:, f, :], HB[f % 2][:, :], ACT.Gelu_apprx_tanh, bias=vec(j - 1, BF1 + f)).then_inc(h_gelu, 1)
                if ok(j - 2) and j % 2 == 0:
                    eng.wait_ge(feat_d[1], n(1) + j - 1)
                    eng.activation(xT[:, tile_of(j - 2)], OB[:, :], ACT.Identity, scale=vec(j - 2, S2C), bias=vec(j - 2, B2C)).then_inc(xo_d[1], 1)
                if ok(j + 6) and j % 2 == 0:
                    wait_input(eng, j + 6, n)
                    eng.activation(xh[:, :], xT[:, tile_of(j + 6)], ACT.Copy).then_inc(xh_d, 1)
                if j % 2:
                    window(j, n)
                if pair(j) is not None:
                    expert_gelus(pair(j), n)
                if ok(j - 1):
                    eng.wait_ge(f2_mm, n(1) + j)
                    eng.activation(O2[:, :], O2[:, :], ACT.Gelu_apprx_tanh, bias=vec(j - 1, BF2)).then_inc(f2_gelu, 1)
                if ok(j) and not by_vector(j):
                    eng.wait_ge(feat_d[0], n(1) + j + 1)
                    eng.activation(x1[:, j % 2, :], OB[:, :], ACT.Identity, scale=vec(j, S1C), bias=vec(j, B1C)).then_inc(xo_d[0], 1)
                    eng.wait_ge(xo_d[0], n(1) + j + 1)
                    eng.activation(x1h[:, :], x1[:, j % 2, :], ACT.Copy).then_inc(x1h_d, 1)
                a = j + 6
                if ok(a) and not by_vector(j):
                    if a >= 4:
                        eng.wait_ge(KV_d, n(1) + a - 3)
                        eng.wait_ge(Q_d, n(1) + a - 3)
                    for c, (dst, b) in enumerate(((kz[:, a % 4, :], BK), (qz[:, a % TILES, :], BQ))):
                        eng.wait_ge(qkv_mm, n(3) + 3 * a + c + 1)
                        eng.activation(dst, QKV[(3 * a + c) % 2][:, :], ACT.Identity, bias=vec(a, b)).then_inc(qkv_ev, 1)

            def window(j, n):
                ap = [a for a in (j + 4, j + 5) if ok(a)]
                sp = [g for g in (j + 1, j + 2) if ok(g)]
                if ap or sp:
                    nc.scalar.preload_act_table_set("natural_log_exp_and_others")
                if ap:
                    eng.wait_ge(min_d, n(2) + 2 * ap[-1] + 2)
                for a in ap:
                    eng.activation(mk[:, a % 4, :], mk[:, a % 4, :], ACT.Exp).then_inc(exp_k, 1)
                for a in ap:
                    eng.activation(mq[:, a % 4, :], mq[:, a % 4, :], ACT.Exp).then_inc(exp_q, 1)
                if j == -3:
                    probabilities()
                for g in sp:
                    eng.wait_ge(Q_d, n(1) + g + 1)
                    if g % SEQ_TILES == 0:
                        eng.wait_ge(coef_d, nseq(g, n))
                    eng.activation(sz[:, g % 4, :], qz[:, g % TILES, :], ACT.Ln, scale=ks[:, seq(g), 2:3], bias=one[:, 0:1]).then_inc(ln_d, 1)
                for g in sp:
                    eng.wait_ge(ln_d, n(1) + g + 1)
                    eng.activation(sz[:, g % 4, :], sz[:, g % 4, :], ACT.Exp, scale=-1.0).then_inc(s_d, 1)
                if ap or sp:
                    nc.scalar.preload_act_table_set("gelu_apprx_tanh_and_others")
            steps(eng, step)

        @block.vector
        def _(eng):
            def input_moments(c):
                eng.wait_ge(in_x[c], 16)
                for t in range(8 * c, 8 * c + 8):
                    last = eng.bn_stats(st0[:, t, :], x0[:, t, :])
                last.then_inc(st0_d, 1)
                eng.wait_ge(st0_d, c + 1)
                for t in range(8 * c, 8 * c + 8):
                    last = eng.bn_aggr(ag0[:, t, :], st0[:, t, :])
                last.then_inc(ag0_d, 1)

            def input_scale(c):
                eng.wait_ge(rs0_d, c + 1)
                for t in range(8 * c, 8 * c + 8):
                    eng.tensor_scalar(xn[:, t, :], x0[:, t, :], ag0[:, t, 0:1], rs0[:, 1, t:t + 1],
                                      ALU.subtract, ALU.mult).then_inc(xn_d, 1)
            input_moments(0)
            for c in range(1, 4):
                input_moments(c)
                input_scale(c - 1)
            input_scale(3)

            chain = [0]

            def link(ins):
                chain[0] += 1
                ins.then_inc(rchain, 1)
                eng.wait_ge(rchain, chain[0])
            lg = B[2][:, 0:TT * E].rearrange("p (t e) -> p t e", e=E)

            def choose():
                eng.wait_ge(logits_d, 1)
                link(eng.tensor_reduce(rmx[:, :], lg, AX.X, ALU.max))
                eng.tensor_tensor(out=rd[:, :, :], in0=lg, in1=rmx[:, :].unsqueeze(2).broadcast_to([P, TT, E]), op=ALU.subtract).then_inc(rdiff, 1)
                eng.wait_ge(rdiff, 1)
                link(eng.tensor_scalar(cand[:, :, :], rd[:, :, :], 0.0, None, ALU.is_ge))
                link(eng.tensor_tensor(out=cand[:, :, :], in0=cand[:, :, :], in1=w8[:, :].unsqueeze(1).broadcast_to([P, TT, E]), op=ALU.mult))
                link(eng.tensor_reduce(cmx[:, :], cand[:, :, :], AX.X, ALU.max))
                link(eng.tensor_tensor(out=oh[:, :, :], in0=cand[:, :, :], in1=cmx[:, :].unsqueeze(2).broadcast_to([P, TT, E]), op=ALU.is_equal))
                eng.tensor_copy(ohb[:, :, :], oh[:, :, :]).then_inc(onehot_d, 1)

            def place():
                eng.wait_ge(counts_d, 1)
                rank = B[4][:, 0:TT * E].rearrange("p (t e) -> p t e", e=E)
                link(eng.tensor_copy(tot[:, :, :], B[3][:, 0:TT * E].rearrange("p (t e) -> p t e", e=E)))
                for e in range(E):
                    last = eng.tensor_tensor_scan(cum[:, :, e], onest[:, :], tot[:, :, e], 0.0, ALU.mult, ALU.add)
                link(last)
                link(eng.tensor_scalar(ntf[:, 0, :], cum[:, TT - 1, :], float(P - 1), None, ALU.add))
                link(eng.tensor_copy(nti[:, 0, :], ntf[:, 0, :]))
                link(eng.tensor_scalar(nti[:, 1, :], nti[:, 0, :], 7, None, ALU.logical_shift_right))
                link(eng.tensor_copy(ntf[:, 1, :], nti[:, 1, :]))
                link(eng.tensor_tensor_scan(ntf[:, 2, :], onest[:, 0:E], ntf[:, 1, :], 0.0, ALU.mult, ALU.add))
                link(eng.tensor_tensor(out=ntf[:, 3, :], in0=ntf[:, 2, :], in1=ntf[:, 1, :], op=ALU.subtract))
                link(eng.tensor_tensor(out=cum[:, :, :], in0=cum[:, :, :], in1=tot[:, :, :], op=ALU.subtract))
                link(eng.tensor_tensor(out=cum[:, :, :], in0=rank, in1=cum[:, :, :], op=ALU.add))
                link(eng.scalar_tensor_tensor(out=cum[:, :, :], in0=ntf[:, 3, :].unsqueeze(1).broadcast_to([P, TT, E]), scalar=float(P),
                                              in1=cum[:, :, :], op0=ALU.mult, op1=ALU.add))
                link(eng.tensor_tensor(out=cum[:, :, :], in0=cum[:, :, :], in1=oh[:, :, :], op=ALU.mult))
                link(eng.tensor_reduce(slf[:, :], cum[:, :, :], AX.X, ALU.add))
                eng.tensor_copy(slot[:, :], slf[:, :]).then_inc(slots_d, 1)

            def experts_of_tiles():
                link(eng.tensor_scalar(exf[:, :], tix[:, :], 0.0, -1.0, ALU.mult, ALU.add))
                for e in range(E):
                    link(eng.scalar_tensor_tensor(out=exf[:, :], in0=tix[:, :], scalar=ntf[0:1, 3, e:e + 1],
                                                  in1=exf[:, :], op0=ALU.is_ge, op1=ALU.add))
                eng.tensor_copy(exi[:, :], exf[:, :]).then_inc(expid_d, 1)

            def probability():
                eng.wait_ge(rexp, 1)
                link(eng.tensor_reduce(psm[:, :], re[:, :, :], AX.X, ALU.add))
                link(eng.reciprocal(pmax[:, :], psm[:, :]))

            def add(g, i, n):
                if i == 0:
                    eng.wait_ge(o_gelu, n(1) + g + 1)
                    eng.tensor_tensor(out=ybuf[:, 0, :], in0=OB[:, :], in1=xT[:, tile_of(g)], op=ALU.add).then_inc(y_d[0], 1)
                else:
                    eng.wait_ge(f2_gelu, n(1) + g + 1)
                    eng.tensor_tensor(out=ybuf[:, 1, :], in0=O2[:, :], in1=x1[:, g % 2, :], op=ALU.add).then_inc(y_d[1], 1)

            def statistics(g, i, n):
                eng.wait_ge(tok_d[i], n(1) + g + 1)
                for c in range(4):
                    last = eng.bn_stats(st[:, i, c, :], TOK[i][:, c * P:(c + 1) * P])
                last.then_inc(bn_d[i], 1)

            def moments(g, i, n):
                eng.wait_ge(in_x[0], 16)
                eng.wait_ge(bn_d[i], n(1) + g + 1)
                for c in range(4):
                    last = eng.bn_aggr(ag[:, i, c, :], st[:, i, c, :])
                last.then_inc(ag_d[i], 1)

            def scale(g, i, n):
                eng.wait_ge(rs_d[i], n(1) + g + 1)
                for c in range(4):
                    last = eng.tensor_scalar(nbuf[:, i, c * P:(c + 1) * P], TOK[i][:, c * P:(c + 1) * P], ag[:, i, c, 0:1],
                                             rstd[:, i, c:c + 1], ALU.subtract, ALU.mult)
                last.then_inc(nrm_d[i], 1)

            def negatives(a, n):
                eng.wait_ge(qkv_ev, n(3) + 3 * a + 1)
                eng.tensor_scalar(mk[:, a % 4, :], kz[:, a % 4, :], 0.0, None, ALU.min).then_inc(min_d, 1)
                eng.wait_ge(qkv_ev, n(3) + 3 * a + 2)
                eng.tensor_scalar(mq[:, a % 4, :], qz[:, a % TILES, :], 0.0, None, ALU.min).then_inc(min_d, 1)

            def sum_k(a, n):
                eng.wait_ge(exp_k, n(1) + a + 1)
                eng.scalar_tensor_tensor(out=mk[:, a % 4, :], in0=kz[:, a % 4, :], scalar=1.0, in1=mk[:, a % 4, :],
                                         op0=ALU.add, op1=ALU.max, accum_out=kp[:, a % TILES:a % TILES + 1]).then_inc(K_d, 1)

            def sum_kv(a, n):
                eng.wait_ge(K_d, n(1) + a + 1)
                eng.wait_ge(qkv_ev, n(3) + 3 * a + 3)
                eng.scalar_tensor_tensor(out=vz[:, a % 4, :], in0=vz[:, a % 4, :], scalar=1.0, in1=mk[:, a % 4, :],
                                         op0=ALU.mult, op1=ALU.mult, accum_out=kvp[:, a % TILES:a % TILES + 1]).then_inc(KV_d, 1)

            def queries(a, n):
                eng.wait_ge(exp_q, n(1) + a + 1)
                eng.tensor_scalar(mq[:, a % 4, :], mq[:, a % 4, :], -1.0, 1.0, ALU.add, ALU.add).then_inc(eq_d, 1)
                eng.wait_ge(eq_d, n(1) + a + 1)
                eng.scalar_tensor_tensor(out=qz[:, a % TILES, :], in0=qz[:, a % TILES, :], scalar=1.0, in1=mq[:, a % 4, :],
                                         op0=ALU.add, op1=ALU.max).then_inc(Q_d, 1)

            def nth(a, k, n):
                return n(1.25) + 5 * (a // SEQ_TILES) + k

            def whole_sum_k(a, n):
                s, first = seq(a), a % TILES - 3
                eng.wait_ge(K_d, n(1) + a + 1)
                eng.tensor_reduce(ks[:, s, 0:1], kp[:, first:first + 4], AX.X, ALU.add).then_inc(cchain, 1)
                eng.wait_ge(cchain, nth(a, 1, n))
                eng.tensor_scalar(ks[:, s, 2:3], ks[:, s, 0:1], 1.0 / EPS_Z, None, ALU.mult).then_inc(coef_d, 1)

            def alpha(a, n):
                s, first = seq(a), a % TILES - 3
                eng.tensor_scalar(ks[:, s, 3:4], ks[:, s, 0:1], 1e-30, None, ALU.max).then_inc(cchain, 1)
                eng.wait_ge(cchain, nth(a, 2, n))
                eng.reciprocal(ks[:, s, 4:5], ks[:, s, 3:4]).then_inc(cchain, 1)
                eng.wait_ge(KV_d, n(1) + a + 1)
                eng.tensor_reduce(ks[:, s, 1:2], kvp[:, first:first + 4], AX.X, ALU.add).then_inc(cchain, 1)
                eng.wait_ge(cchain, nth(a, 4, n))
                eng.tensor_tensor(out=ks[:, s, 5:6], in0=ks[:, s, 1:2], in1=ks[:, s, 4:5], op=ALU.mult).then_inc(cchain, 1)
                eng.wait_ge(cchain, nth(a, 5, n))
                eng.tensor_scalar(nwo[:, s, :], w[:, lay(a), CO:CO + D], ks[:, s, 5:6], -1.0, ALU.mult, ALU.mult).then_inc(nwo_d, 1)

            def finish(g):
                if g == 0:
                    eng.wait_ge(gathered, 16 * TT)
                eng.wait_ge(fin_T, 4 * (g + 1))
                if g >= 4:
                    eng.wait_ge(fin_st[g % 4], 16)
                eng.tensor_tensor(out=res[:, g % 4, :, :], in0=QKV[g % 2][:, :].rearrange("p (a d) -> p a d", a=4),
                                  in1=x0[:, 4 * g:4 * g + 4, :], op=ALU.add).then_inc(fin_r1, 1)
                eng.wait_ge(fin_r1, g + 1)
                for c in range(4):
                    t = 4 * g + c
                    eng.scalar_tensor_tensor(out=res[:, g % 4, c, :], in0=xg[:, t, :], scalar=pmax[:, t:t + 1],
                                             in1=res[:, g % 4, c, :], op0=ALU.mult, op1=ALU.add).then_inc(fin_r2, 1)

            def step(j, n):
                a, p, g, b = j + 6, pair(j), j + 1, j + 4
                if ok(j) and j % SEQ_TILES == 0:
                    eng.wait_ge(bo_mm, nseq(j, n))
                    eng.tensor_scalar(bo2[:, seq(j):seq(j) + 1], TOK[0][:, 0:1], vec(j, BO), None, ALU.add).then_inc(bo_d, 1)
                if ok(j):
                    add(j, 0, n)
                if ok(j - 2):
                    statistics(j - 2, 1, n)
                if ok(j - 2):
                    moments(j - 2, 1, n)
                if ok(j):
                    statistics(j, 0, n)
                    moments(j, 0, n)
                if pair(j - 1) is not None:
                    d = pair(j - 1)
                    eng.wait_ge(m_f2, n(PTURN / 16) + d + 1)
                    if d >= 1:
                        eng.wait_ge(m_st, n(6) + 16 * d)
                    eng.tensor_copy(my[:, :, :], QKV[a % 2][:, 0:2 * D].rearrange("p (i d) -> p i d", i=2)).then_inc(m_y, 1)
                if ok(j - 2):
                    scale(j - 2, 1, n)
                if p is not None:
                    eng.wait_ge(m_T, n(PTURN / 16) + p + 1)
                    eng.tensor_copy(mxT[:, :, :], QKV[a % 2][:, 0:2 * P].rearrange("p (i t) -> p i t", i=2)).then_inc(m_xT, 1)
                if ok(b) and b % SEQ_TILES == 3:
                    sum_k(b, n)
                    whole_sum_k(b, n)
                if j % 2:
                    if ok(j - 2):
                        eng.wait_ge(feat_d[1], n(1) + j - 1)
                        eng.tensor_scalar(xT[:, tile_of(j - 2)], OB[:, :], vec(j - 2, S2C), vec(j - 2, B2C), ALU.mult, ALU.add).then_inc(xo_d[1], 1)
                    if ok(a):
                        wait_input(eng, a, n)
                        eng.tensor_copy(xh[:, :], xT[:, tile_of(a)]).then_inc(xh_d, 1)
                if ok(j):
                    scale(j, 0, n)
                if ok(b) and j % 2:
                    if b % SEQ_TILES == 3:
                        sum_kv(b, n)
                    else:
                        sum_k(b, n)
                if j % 2 == 0:
                    if ok(b):
                        sum_k(b, n)
                        sum_kv(b, n)
                    for i in (b - 1, b):
                        if ok(i):
                            queries(i, n)
                if ok(j) and by_vector(j):
                    eng.wait_ge(feat_d[0], n(1) + j + 1)
                    eng.tensor_scalar(x1[:, j % 2, :], OB[:, :], vec(j, S1C), vec(j, B1C), ALU.mult, ALU.add).then_inc(xo_d[0], 1)
                    eng.wait_ge(xo_d[0], n(1) + j + 1)
                    eng.tensor_copy(x1h[:, :], x1[:, j % 2, :]).then_inc(x1h_d, 1)
                if ok(a) and by_vector(j):
                    if a >= 4:
                        eng.wait_ge(KV_d, n(1) + a - 3)
                    eng.wait_ge(qkv_ev, n(3) + 3 * a)
                    eng.wait_ge(qkv_mm, n(3) + 3 * a + 1)
                    eng.tensor_scalar(kz[:, a % 4, :], bank(a, 0), vec(a, BK), None, ALU.add).then_inc(qkv_ev, 1)
                if ok(b) and b % SEQ_TILES == 3:
                    alpha(b, n)
                if ok(a) and by_vector(j):
                    eng.wait_ge(qkv_mm, n(3) + 3 * a + 2)
                    eng.tensor_scalar(qz[:, a % TILES, :], bank(a, 1), vec(a, BQ), None, ALU.add).then_inc(qkv_ev, 1)
                if ok(b) and j % 2 and b % SEQ_TILES != 3:
                    sum_kv(b, n)
                if ok(a - 1) and j % 2 == 0 and p is None:
                    negatives(a - 1, n)
                if j == -6:
                    choose()
                if j == -4:
                    place()
                if j == -3:
                    probability()
                if j == -2:
                    experts_of_tiles()
                if ok(j - 1):
                    add(j - 1, 1, n)
                if ok(a - 1) and j % 2 == 0 and p is not None:
                    negatives(a - 1, n)
                if ok(a) and j % 2 == 0:
                    negatives(a, n)
                for i in finished(j):
                    finish(i)
            steps(eng, step)
            finish(TILES - 1)

        @block.tensor
        def _(eng):
            def logits(first, last):
                eng.wait_ge(in_r, 16)
                for t in range(first, last):
                    eng.wait_ge(xT_d, t // 4 + 1)
                    product = eng.matmul(B[2][:, t * E:(t + 1) * E], xT[:, t * P:(t + 1) * P], wrs[:, :], start=True, stop=True)
                if last == TT:
                    product.then_inc(logits_d, 1)

            eng.wait_ge(consts, 12)
            for g in range(TILES):
                eng.wait_ge(xn_d, 4 * (g + 1))
                if g >= 2:
                    eng.wait_ge(xT_d, g - 1)
                for c in range(4):
                    eng.transpose(B[g % 2][:, c * P:(c + 1) * P], xn[:, 4 * g + c, :], ident[:, :]).then_inc(xn_T, 1)
                if g >= 1:
                    logits(4 * g - 4, 4 * g)
            logits(TT - 4, TT)

            def counts():
                eng.wait_ge(onehot_d, 1)
                ohv = ohb[:, :, :].rearrange("p t e -> p (t e)")
                eng.matmul(B[3][:, 0:TT * E], onesb[:, :], ohv, start=True, stop=True)
                eng.matmul(B[4][:, 0:TT * E], tri[:, :], ohv, start=True, stop=True).then_inc(counts_d, 1)

            def W(i, c, width=D):
                return w[:, lay(i), c:c + width]

            def to_tokens(g, i, n):
                eng.wait_ge(y_d[i], n(1) + g + 1)
                if g >= 1:
                    eng.wait_ge(nrm_d[i], n(1) + g)
                for c in range(4):
                    last = eng.transpose(TOK[i][:, c * P:(c + 1) * P], ybuf[:, i, c * P:(c + 1) * P], ident[:, :])
                last.then_inc(tok_d[i], 1)

            def to_features(g, i, n):
                eng.wait_ge(nrm_d[i], n(1) + g + 1)
                if i == 0 and g >= 2:
                    eng.wait_ge(xo_d[1], n(1) + g - 1)
                if i == 1 and g + 2 >= STEPS:
                    eng.wait_ge(xo_d[0], STEPS)
                    eng.wait_ge(xo_d[1], g)
                for c in range(4):
                    last = eng.transpose(OB[:, c * P:(c + 1) * P], nbuf[:, i, c * P:(c + 1) * P], ident[:, :])
                last.then_inc(feat_d[i], 1)

            def of_upper(out, i, c, high):
                eng.matmul(out, wh[:, lay(i), c:c + P], high, start=True, stop=False)
                eng.matmul(out, wl[:, lay(i), c:c + P], high, start=False, stop=False)

            def of_lower(out, i, c, low):
                return eng.matmul(out, wh[:, lay(i), c:c + P], low, start=False, stop=True)

            def expert_rows(p, a, n):
                for i in range(2):
                    eng.wait_ge(m_w[i], n(18) + 48 * p + 48)
                eng.wait_ge(qkv_ev, n(3) + 3 * a - 1)
                for i in range(2):
                    last = eng.transpose(QKV[a % 2][:, i * P:(i + 1) * P], mx[:, i, :], ident[:, :])
                last.then_inc(m_T, 1)

            def expert_up(p, n):
                eng.wait_ge(m_xT, n(PTURN / 16) + p + 1)
                for i in range(2):
                    for f in range(FC):
                        last = eng.matmul(HB[i][:, f * P:(f + 1) * P], wm[:, i, f * P:(f + 1) * P], mxT[:, i, :],
                                          start=True, stop=True)
                    last.then_inc(m_f1, 1)

            def expert_down(p, a, i, n):
                if i == 0:
                    eng.wait_ge(qkv_ev, n(3) + 3 * a + 2)
                for f in range(FC):
                    eng.matmul(QKV[(a + 1) % 2][:, i * D:(i + 1) * D], mh[:, i, f, :], wm[:, i, F + f * D:F + (f + 1) * D],
                               start=(f == 0), stop=False)
                last = eng.matmul(QKV[(a + 1) % 2][:, i * D:(i + 1) * D], ones_r[:, :], b2r[:, i, :], start=False, stop=True)
                if i == 1:
                    last.then_inc(m_f2, 1)

            def project(a, n):
                if a % TILES == 0:
                    eng.wait_ge(in_w[lay(a)], n(1) + a // (2 * TILES) * 16 + 16)
                    eng.wait_ge(wl_d, n(0.125) + a // TILES + 1)
                eng.wait_ge(xh_d, n(1) + a + 1)
                for c in range(2):
                    if 3 * a + c >= 2:
                        eng.wait_ge(qkv_ev, n(3) + 3 * a + c - 1)
                    of_upper(bank(a, c), a, (CK, CQ)[c], xh[:, :])

            def project_lower(a, n):
                eng.wait_ge(xl_d, n(1) + a + 1)
                for c in range(2):
                    of_lower(bank(a, c), a, (CK, CQ)[c], xl[:, :]).then_inc(qkv_mm, 1)

            def project_v(a, n):
                eng.wait_ge(qkv_ev, n(3) + 3 * a + 1)
                of_upper(bank(a, 2), a, CV, xh[:, :])
                of_lower(bank(a, 2), a, CV, xl[:, :]).then_inc(qkv_mm, 1)

            def hidden(g, f, n):
                for c in (f, f + 1):
                    if 4 * g + c >= 2:
                        eng.wait_ge(h_gelu, n(4) + 4 * g + c - 1)
                    of_upper(HB[c % 2][:, :], g, CF1 + c * P, x1h[:, :])
                if f == 0:
                    eng.wait_ge(x1l_d, n(1) + g + 1)
                for c in (f, f + 1):
                    of_lower(HB[c % 2][:, :], g, CF1 + c * P, x1l[:, :]).then_inc(h_mm, 1)

            def last_transposes(g):
                eng.wait_ge(xo_d[1], STEPS - TILES + g + 1)
                if g < 2:
                    eng.wait_ge(qkv_ev, 3 * STEPS)
                else:
                    eng.wait_ge(fin_r1, g - 1)
                for c in range(4):
                    eng.transpose(QKV[g % 2][:, c * P:(c + 1) * P], xT[:, g * TS + c * P:g * TS + (c + 1) * P], ident[:, :]).then_inc(fin_T, 1)

            def step(j, n):
                a, p, g = j + 6, pair(j), j - 1
                def attend():
                    eng.wait_ge(s_d, n(1) + j + 1)
                    if j % SEQ_TILES == 0:
                        eng.wait_ge(nwo_d, nseq(j, n))
                    if j >= 1:
                        eng.wait_ge(xo_d[0], n(1) + j)
                    eng.matmul(OB[:, :], nwo[:, seq(j), :], sz[:, j % 4, :], start=True, stop=True).then_inc(o_mm, 1)

                if ok(j) and j % SEQ_TILES != 0:
                    attend()
                if ok(a - 1):
                    project_v(a - 1, n)
                if ok(g):
                    eng.wait_ge(x1h_d, n(1) + g + 1)
                    if pair(j - 1) is not None:
                        eng.wait_ge(m_h, n(PTURN / 16) * 2 + 2 * pair(j - 1) + 2)
                    hidden(g, 0, n)
                if ok(j) and j % SEQ_TILES == 0:
                    eng.wait_ge(nwo_d, nseq(j, n))
                    if j >= 1:
                        eng.wait_ge(nrm_d[0], n(1) + j)
                    eng.matmul(TOK[0][:, 0:1], W(j, CO), ks[:, seq(j), 5:6], start=True, stop=True).then_inc(bo_mm, 1)
                    attend()
                if ok(j - 2):
                    to_tokens(j - 2, 1, n)
                if pair(j - 1) is not None:
                    expert_down(pair(j - 1), a - 1, 0, n)
                if ok(j):
                    to_tokens(j, 0, n)
                if ok(g):
                    hidden(g, 2, n)
                if pair(j - 1) is not None:
                    expert_down(pair(j - 1), a - 1, 1, n)
                if p is not None:
                    expert_rows(p, a, n)
                if ok(g) and g >= 1:
                    eng.wait_ge(y_d[1], n(1) + g)
                for f in range(FC):
                    if f == 2:
                        if ok(j - 2):
                            to_features(j - 2, 1, n)
                        if p is not None:
                            if ok(g):
                                eng.wait_ge(h_gelu, n(4) + 4 * g + FC)
                            expert_up(p, n)
                    if ok(g):
                        eng.wait_ge(h_gelu, n(4) + 4 * g + f + 1)
                        last = eng.matmul(O2[:, :], W(g, CF2 + f * D), hb[:, f, :], start=(f == 0), stop=(f == FC - 1))
                        if f == FC - 1:
                            last.then_inc(f2_mm, 1)
                if ok(j) and not j % 2:
                    to_features(j, 0, n)
                if ok(a):
                    if pair(j - 1) is not None:
                        eng.wait_ge(m_y, n(PTURN / 16) + pair(j - 1) + 1)
                    project(a, n)
                if ok(j) and j % 2:
                    to_features(j, 0, n)
                if ok(a):
                    project_lower(a, n)
                if j == -5:
                    counts()
                for i in finished(j):
                    last_transposes(i)
            steps(eng, step)
            last_transposes(TILES - 1)


def kernel(**inputs):
    import numpy as np
    import concourse.bacc as bacc
    from concourse import mybir as mb
    from concourse.bass_utils import run_bass_kernel_spmd as run

    a = {k: np.asarray(v) for k, v in inputs.items()}
    at = {k[8:]: v for k, v in a.items() if k.startswith("L0_attn_")}
    ff = {k[7:]: v for k, v in a.items() if k.startswith("L0_ffn_")}
    vecs = [at[n][:, :, None] for n in ("bq", "bk", "bv", "bo", "ln1_s", "ln1_b", "bf2", "ln2_s", "ln2_b")]
    wf2 = at["Wf2"].reshape(L, FC, P, D).transpose(0, 2, 1, 3).reshape(L, P, FC * D)
    bf1 = at["bf1"].reshape(L, FC, P).transpose(0, 2, 1)
    spack = np.ascontiguousarray(np.concatenate([at["Wq"], at["Wk"], at["Wv"], at["Wf1"]], axis=2))
    wpack = np.ascontiguousarray(np.concatenate([at["Wo"], wf2, *vecs, bf1], axis=2))
    w2 = ff["W2"].reshape(E, FC, P, D).transpose(0, 2, 1, 3).reshape(E, P, FC * D)
    mpack = np.ascontiguousarray(np.concatenate([ff["W1"], w2, ff["b1"].reshape(E, FC, P).transpose(0, 2, 1)], axis=2))
    arrays = {"x": np.ascontiguousarray(at["x"]).reshape(T, D), "spack": spack, "wpack": wpack, "wr": np.ascontiguousarray(ff["Wr"]),
              "mpack": mpack, "b2": np.ascontiguousarray(ff["b2"])}
    nc = bacc.Bacc("TRN2", target_bir_lowering=False, num_devices=1)
    args = [nc.dram_tensor(n, v.shape, mb.dt.from_np(v.dtype), kind="ExternalInput").ap() for n, v in arrays.items()]
    o = nc.dram_tensor("out", (T, D), mb.dt.float32, kind="ExternalOutput").ap()
    build(nc, *args, o)
    r = run(nc, [arrays], core_ids=[0])
    return r.results[0]["out"].reshape(2, T // 2, D)
```
